# Optimizing a Trainium2 kernel written in Bass

```python
import numpy as np
import jax
import jax.numpy as jnp

def _softmax(x, axis=-1):
    return jax.nn.softmax(x, axis=axis)

def _gelu(x):
    return jax.nn.gelu(x, approximate=True)

def _silu(x):
    return jax.nn.silu(x)

def _sigmoid(x):
    return jax.nn.sigmoid(x)

def _layernorm(x, axis=-1, eps=1e-05):
    m = jnp.mean(x, axis=axis, keepdims=True)
    v = jnp.var(x, axis=axis, keepdims=True)
    return (x - m) / jnp.sqrt(v + eps)

def _scatter_add(tgt, idx, src, axis=0):
    return tgt.at[idx].add(src)

def _segment_sum(src, seg, n):
    return jax.ops.segment_sum(src, seg, n)
kernel_name = 'mk_flamingo_gated_d1_seqx_r8_4635b0'

def setup_inputs(seed: int=0):
    np.random.seed(seed)
    _w = jnp.asarray

    def _rec_inputs():
        import jax
        import jax.numpy as jnp
        _rk = jax.random.key(seed)
        x = -0.0002928 + 1 * jax.random.normal(jax.random.fold_in(_rk, 1), (4, 256, 128), jnp.float32)
        _lenS = 256 - jax.random.randint(jax.random.fold_in(_rk, 7), (4,), 0, max(1, 256 // 4) + 1, jnp.int32)
        _lenS2 = 256 - jax.random.randint(jax.random.fold_in(_rk, 8), (4,), 0, max(1, 256 // 4) + 1, jnp.int32)
        _ctx_1024P = jax.random.normal(jax.random.fold_in(_rk, 11), (4, 16, 128), jnp.float32)
        _ctx_1024c = jax.random.dirichlet(jax.random.fold_in(_rk, 511), 0.3 * jnp.ones((16,), jnp.float32), (4, 256))
        _ctx_1024t = jnp.einsum('bsk,bkd->bsd', _ctx_1024c, _ctx_1024P)
        _ctx_1024t = _ctx_1024t * jax.lax.rsqrt(jnp.mean(jnp.square(_ctx_1024t)) + 1e-12) * 0.953939
        ctx_1024 = -1.39393e-06 + 0.999914 * (_ctx_1024t + 0.3 * jax.random.normal(jax.random.fold_in(_rk, 611), (4, 256, 128), jnp.float32))
        _g = jax.random.normal(jax.random.fold_in(_rk, 9001), (2, 1), jnp.float32)
        _g = jnp.sign(_g) * jnp.maximum(jnp.abs(_g), 1.0) + (_g == 0) * 1.0
        g_xattn = _g[0]
        g_ffn = _g[1]
        return (x, ctx_1024, g_xattn, g_ffn)
    x, ctx_1024, g_xattn, g_ffn = _rec_inputs()

    def _L0_xattn_setup():
        import jax, jax.numpy as jnp
        import numpy as np
        B, S, D, NH = (2, 256, 128, 8)
        DH = D // NH
        EPS = 1e-06
        LN_EPS = 1e-05

        def _mlstm_cell(q, k, v, igate_w, igate_b, fgate_w, fgate_b, ln_scale):
            Slen = q.shape[0]
            ifg = jnp.concatenate([q, k, v], axis=-1)
            ig = (ifg @ igate_w.T + igate_b).T
            fg = (ifg @ fgate_w.T + fgate_b).T
            qh = q.reshape(Slen, NH, DH).transpose(1, 0, 2)
            kh = k.reshape(Slen, NH, DH).transpose(1, 0, 2)
            vh = v.reshape(Slen, NH, DH).transpose(1, 0, 2)
            log_f = jax.nn.log_sigmoid(fg)
            cs = jnp.cumsum(log_f, axis=1)
            fg_mat = cs[:, :, None] - cs[:, None, :]
            mask = jnp.tril(jnp.ones((Slen, Slen), dtype=bool))
            log_fg_mat = jnp.where(mask, fg_mat, -jnp.inf)
            log_D = log_fg_mat + ig[:, None, :]
            max_log_D = jnp.max(log_D, axis=-1, keepdims=True)
            D_mat = jnp.exp(log_D - max_log_D)
            qk = jnp.einsum('hsd,htd->hst', qh, kh) / np.sqrt(DH)
            C = qk * D_mat
            normalizer = jnp.maximum(jnp.abs(C.sum(axis=-1, keepdims=True)), jnp.exp(-max_log_D))
            h = jnp.einsum('hst,htd->hsd', C / (normalizer + EPS), vh)
            h = h.transpose(1, 0, 2).reshape(Slen, D)
            mu = h.mean(axis=-1, keepdims=True)
            var = h.var(axis=-1, keepdims=True)
            return (h - mu) / jnp.sqrt(var + LN_EPS) * ln_scale
        key = jax.random.key(seed)
        ks = jax.random.split(key, 8)
        rnd = lambda k, sh, s=1.0: jax.random.normal(k, sh, dtype=jnp.float32) * s
        return {'q': rnd(ks[0], (B, S, D)), 'k': rnd(ks[1], (B, S, D)), 'v': rnd(ks[2], (B, S, D)), 'igate_w': rnd(ks[3], (NH, 3 * D), 0.02), 'igate_b': jnp.linspace(3.0, 6.0, NH, dtype=jnp.float32), 'fgate_w': rnd(ks[4], (NH, 3 * D), 0.02), 'fgate_b': rnd(ks[5], (NH,), 0.3162278), 'ln_scale': jnp.ones((D,), dtype=jnp.float32)}
    _L0_xattn_all = _L0_xattn_setup()
    _L0_xattn_in = {k: v for k, v in _L0_xattn_all.items() if k in ('igate_w', 'igate_b', 'fgate_w', 'fgate_b', 'ln_scale')}
    del _L0_xattn_all

    def _L0_ffn_setup():
        import jax, jax.numpy as jnp
        import numpy as np
        B, S, D = (4, 256, 128)
        E, F = (8, 512)
        key = jax.random.key(seed)
        ks = jax.random.split(key, 5)
        x = jax.random.normal(ks[0], (B, S, D), dtype=jnp.float32)
        switch_w = jax.random.normal(ks[1], (D, E), dtype=jnp.float32) * D ** (-0.5)
        switch_b = jnp.zeros((E,), dtype=jnp.float32)
        w1 = jax.random.normal(ks[2], (E, D, F), dtype=jnp.float32) * D ** (-0.5)
        b1 = jnp.zeros((E, F), dtype=jnp.float32)
        w2 = jax.random.normal(ks[3], (E, F, D), dtype=jnp.float32) * F ** (-0.5)
        b2 = jnp.zeros((E, D), dtype=jnp.float32)
        return {'x': x, 'switch_w': switch_w, 'switch_b': switch_b, 'w1': w1, 'b1': b1, 'w2': w2, 'b2': b2}
    _L0_ffn_all = _L0_ffn_setup()
    _L0_ffn_in = {k: v for k, v in _L0_ffn_all.items() if k in ('switch_w', 'switch_b', 'w1', 'b1', 'w2', 'b2')}
    del _L0_ffn_all
    return {'x': x, 'ctx_1024': ctx_1024, 'g_xattn': g_xattn, 'g_ffn': g_ffn, 'L0_xattn_igate_w': _L0_xattn_in['igate_w'], 'L0_xattn_igate_b': _L0_xattn_in['igate_b'], 'L0_xattn_fgate_w': _L0_xattn_in['fgate_w'], 'L0_xattn_fgate_b': _L0_xattn_in['fgate_b'], 'L0_xattn_ln_scale': _L0_xattn_in['ln_scale'], 'L0_ffn_switch_w': _L0_ffn_in['switch_w'], 'L0_ffn_switch_b': _L0_ffn_in['switch_b'], 'L0_ffn_w1': _L0_ffn_in['w1'], 'L0_ffn_b1': _L0_ffn_in['b1'], 'L0_ffn_w2': _L0_ffn_in['w2'], 'L0_ffn_b2': _L0_ffn_in['b2']}

def reference(x, ctx_1024, g_xattn, g_ffn, L0_xattn_igate_w, L0_xattn_igate_b, L0_xattn_fgate_w, L0_xattn_fgate_b, L0_xattn_ln_scale, L0_ffn_switch_w, L0_ffn_switch_b, L0_ffn_w1, L0_ffn_b1, L0_ffn_w2, L0_ffn_b2):
    import jax
    import jax.numpy as jnp

    def _L0_xattn_ref(q, k, v, igate_w, igate_b, fgate_w, fgate_b, ln_scale):
        import jax, jax.numpy as jnp
        import numpy as np
        B, S, D, NH = (2, 256, 128, 8)
        DH = D // NH
        EPS = 1e-06
        LN_EPS = 1e-05

        def _mlstm_cell(q, k, v, igate_w, igate_b, fgate_w, fgate_b, ln_scale):
            Slen = q.shape[0]
            ifg = jnp.concatenate([q, k, v], axis=-1)
            ig = (ifg @ igate_w.T + igate_b).T
            fg = (ifg @ fgate_w.T + fgate_b).T
            qh = q.reshape(Slen, NH, DH).transpose(1, 0, 2)
            kh = k.reshape(Slen, NH, DH).transpose(1, 0, 2)
            vh = v.reshape(Slen, NH, DH).transpose(1, 0, 2)
            log_f = jax.nn.log_sigmoid(fg)
            cs = jnp.cumsum(log_f, axis=1)
            fg_mat = cs[:, :, None] - cs[:, None, :]
            mask = jnp.tril(jnp.ones((Slen, Slen), dtype=bool))
            log_fg_mat = jnp.where(mask, fg_mat, -jnp.inf)
            log_D = log_fg_mat + ig[:, None, :]
            max_log_D = jnp.max(log_D, axis=-1, keepdims=True)
            D_mat = jnp.exp(log_D - max_log_D)
            qk = jnp.einsum('hsd,htd->hst', qh, kh) / np.sqrt(DH)
            C = qk * D_mat
            normalizer = jnp.maximum(jnp.abs(C.sum(axis=-1, keepdims=True)), jnp.exp(-max_log_D))
            h = jnp.einsum('hst,htd->hsd', C / (normalizer + EPS), vh)
            h = h.transpose(1, 0, 2).reshape(Slen, D)
            mu = h.mean(axis=-1, keepdims=True)
            var = h.var(axis=-1, keepdims=True)
            return (h - mu) / jnp.sqrt(var + LN_EPS) * ln_scale
        return jax.vmap(lambda qq, kk, vv: _mlstm_cell(qq, kk, vv, igate_w, igate_b, fgate_w, fgate_b, ln_scale))(q, k, v)

    def _L0_ffn_ref(x, switch_w, switch_b, w1, b1, w2, b2):
        import jax, jax.numpy as jnp
        import numpy as np
        B, S, D = (4, 256, 128)
        E, F = (8, 512)
        b, s, d = x.shape
        t = x.reshape(-1, d)
        logits = t @ switch_w + switch_b
        route_prob = jax.nn.softmax(logits, axis=-1)
        route_prob_max = jnp.max(route_prob, axis=-1)
        routes = jnp.argmax(route_prob, axis=-1)
        out = jnp.zeros_like(t)
        n_experts = w1.shape[0]
        for e in range(n_experts):
            h = jax.nn.gelu(t @ w1[e] + b1[e])
            y = h @ w2[e] + b2[e]
            mask = (routes == e)[:, None]
            out = jnp.where(mask, y, out)
        out = out * route_prob_max[:, None]
        return out.reshape(b, s, d)
    x = x + jnp.tanh(g_xattn[0]) * _L0_xattn_ref(_layernorm(x, axis=-1), ctx_1024, ctx_1024, L0_xattn_igate_w, L0_xattn_igate_b, L0_xattn_fgate_w, L0_xattn_fgate_b, L0_xattn_ln_scale)
    x = x + jnp.tanh(g_ffn[0]) * _L0_ffn_ref(_layernorm(x, axis=-1), L0_ffn_switch_w, L0_ffn_switch_b, L0_ffn_w1, L0_ffn_b1, L0_ffn_w2, L0_ffn_b2)
    return x

_drawn_inputs = setup_inputs


def setup_inputs(seed=0):
    import zlib

    import numpy as np

    out = dict(_drawn_inputs(seed))
    spreads = {'L0_xattn_ln_scale': (1.0, 0.2),
     'L0_ffn_switch_b': (0.0, 0.1),
     'L0_ffn_b1': (0.0, 0.468),
     'L0_ffn_b2': (0.0, 0.32)}
    factors = {}
    for name, (base, spread) in spreads.items():
        noise = np.random.default_rng([zlib.crc32(name.encode()), seed]).standard_normal(out[name].shape)
        drawn = base * np.exp(spread * noise) if base else spread * noise
        out[name] = jnp.asarray(drawn.astype(out[name].dtype))
    for name, factor in factors.items():
        out[name] = (out[name] * factor).astype(out[name].dtype)
    return out
```

```python
from contextlib import ExitStack

import concourse.bass as bass
from concourse import mybir
from concourse.alu_op_type import AluOpType as ALU

ACT = mybir.ActivationFunctionType
F32 = mybir.dt.float32
BF16 = mybir.dt.bfloat16
I32 = mybir.dt.int32
X = mybir.AxisListType.X

P = 128
NEG = -1e30
LN_EPS = 1e-5
EPS = 1e-6


def gated_block(nc, x, ctx_in, g_x, g_f, igw, igb, fgw, fgb, lns, sw, sb_, w1, b1, w2, b2, out):
    B, S, D = x.shape
    H = igw.shape[0]
    DH = D // H
    E, _, F = w1.shape
    NT = B * S // P
    G = H // 4
    U = NT * G
    FJ = F // P
    VW = 32
    BLOCKS = (B * S + E * (P - 1)) // P
    PLW = 2 * D + 8
    assert D == P and S == 2 * P and DH == 16 and FJ == 4

    ctx = ExitStack()
    with ctx:
        def sb(name, shape, dt=F32):
            return ctx.enter_context(nc.sbuf_tensor(name, shape, dt))

        def sem(name):
            return ctx.enter_context(nc.semaphore(name))

        bank = [ctx.enter_context(nc.psum_tensor(f"bank{i}", [P, 512], F32)) for i in range(8)]
        payload = nc.dram_tensor("payload", (B * S, PLW), F32, kind="Internal").ap()

        x_sb = sb("x_sb", [P, NT, D])
        c_sb = sb("c_sb", [P, NT, D])
        gw_rows = sb("gw_rows", [64, 3 * D])
        gbias = sb("gbias", [P, 2])
        gate = sb("gate", [P, 2])
        lnsr = sb("lnsr", [P, D])
        sw_sb = sb("sw_sb", [P, E])
        sbr = sb("sbr", [P, E])
        b1_rows = sb("b1_rows", [E * FJ, P])
        b2r = sb("b2r", [P, E * D])
        w1_sb = sb("w1_sb", [P, E * F])
        w2_sb = sb("w2_sb", [P, E * F])
        identf = sb("identf", [P, P])
        identb = sb("identb", [P, P], BF16)
        selt = sb("selt", [P, B, 3, H])
        sels = sb("sels", [P, B, H])
        sel = sb("sel", [P, B, H, P], BF16)
        mask = sb("mask", [P, 512], BF16)
        bd = sb("bd", [P, H * VW])
        upper = sb("upper", [P, P], BF16)
        ones = sb("ones", [P, P], BF16)
        ci = sb("ci", [P, P], I32)
        cf = sb("cf", [P, P])
        c128 = sb("c128", [P, 16])
        pi = sb("pi", [P, 1], I32)
        dec = sb("dec", [P, E])
        reset = sb("reset", [P, E, NT])
        cv = sb("cv", [P, NT, 3])
        jrow = sb("jrow", [P, 1], I32)
        negk = sb("negk", [P, 2])
        tg = sb("tg", [P, 2])
        g1r = sb("g1r", [P, D])
        st = sb("st", [P, NT, 6])
        mv = sb("mv", [P, NT, 2])
        lnv = sb("lnv", [P, NT])
        rstd = sb("rstd", [P, NT])
        xn = sb("xn", [P, NT, D])
        gwT = sb("gwT", [P, 2, 64])
        b1T = sb("b1T", [P, E * FJ])
        kT = sb("kT", [P, NT * P])
        qT = sb("qT", [P, NT * P])
        qbd = sb("qbd", [P, H, NT * P])
        vaug = sb("vaug", [P, NT, H, VW])
        fmin = sb("fmin", [P, S])
        fabs = sb("fabs", [P, S])
        fexp = sb("fexp", [P, S])
        fln = sb("fln", [P, S])
        cs = sb("cs", [P, S])
        am = sb("am", [P, 2, S])
        nega = sb("nega", [P, S])
        s0 = sb("s0", [P, 2 * S], BF16)
        r1 = sb("r1", [P, 2 * S])
        s1 = sb("s1", [P, 2 * S], BF16)
        spl = sb("spl", [P, 2, S], BF16)
        m1 = sb("m1", [P, 1])
        nm = sb("nm", [P, S])
        ewn = sb("ewn", [P, 4 * P])
        tk = sb("tk", [P, 4, P])
        ek = sb("ek", [P, B, D])
        qw = sb("qw", [P, B, D])
        s1bd = sb("s1bd", [P, 2, H * VW])
        qwT = sb("qwT", [P, 2, P])
        dmat = sb("dmat", [P, 2, 512])
        ct = sb("ct", [P, 2, 512])
        osb = sb("osb", [P, 2, 2 * P])
        nrm = sb("nrm", [P, 4, H])
        hh = sb("hh", [P, NT, D])
        hst = sb("hst", [P, NT, 6])
        hmv = sb("hmv", [P, NT, 2])
        hln = sb("hln", [P, NT])
        hrs = sb("hrs", [P, NT])
        tmp = sb("tmp", [P, 2, D])
        pl = sb("pl", [P, NT, PLW])
        st2 = sb("st2", [P, NT, 6])
        mv2 = sb("mv2", [P, NT, 2])
        ln2 = sb("ln2", [P, NT])
        rs2 = sb("rs2", [P, NT])
        xnT = sb("xnT", [P, NT * P])
        lg = sb("lg", [P, NT, E])
        mx = sb("mx", [P, NT])
        lm = sb("lm", [P, NT, E])
        ex = sb("ex", [P, NT, E])
        sm = sb("sm", [P, NT])
        rsm = sb("rsm", [P, NT])
        enc = sb("enc", [P, NT, E])
        first = sb("first", [P, NT])
        oh = sb("oh", [P, NT, E], BF16)
        cnt = sb("cnt", [P, E, NT])
        incl = sb("incl", [P, E, NT])
        gtk = sb("gtk", [P, E, 8])
        nb = sb("nb", [P, E])
        bend = sb("bend", [P, E])
        bst = sb("bst", [P, E])
        base = sb("base", [P, E, NT])
        t1 = sb("t1", [P, NT, E])
        t2 = sb("t2", [P, NT, E])
        slot = sb("slot", [P, NT])
        gek = sb("gek", [P, NT, 16])
        blk = sb("blk", [P, NT])
        ohb = sb("ohb", [P, NT, 16])
        off = sb("off", [P, NT])
        ohoff = sb("ohoff", [P, NT, P], BF16)
        rv = sb("rv", [P, NT, 3, 16], BF16)
        inv = sb("inv", [P, 3, 16])
        tok = sb("tok", [P, 16])
        pad = sb("pad", [P, 16])
        gidx = sb("gidx", [P, 16], I32)
        sidx = sb("sidx", [P, 16], I32)
        ebc = sb("ebc", [P, 16, E])
        ebf = sb("ebf", [P, 16])
        ebi = sb("ebi", [P, 16], I32)
        xg = sb("xg", [P, BLOCKS, PLW])
        xsT = sb("xsT", [P, 2, P])
        hid = sb("hid", [P, 2, F])
        hT = sb("hT", [P, 2, FJ, P])
        y1 = sb("y1", [P, 2, D])
        yo = sb("yo", [P, BLOCKS, D])

        x_in = [sem("x_in0"), sem("x_in1")]; c_in = sem("c_in"); gw_in = sem("gw_in"); gb_in = sem("gb_in")
        gate_in = sem("gate_in"); lns_in = sem("lns_in"); sw_in = sem("sw_in"); b_in = sem("b_in")
        w1_in = sem("w1_in"); w2_in = sem("w2_in"); qbd_in = sem("qbd_in")
        pl_out = sem("pl_out"); xg_in = [sem(f"xg_in{i}") for i in range(BLOCKS)]; y_out = sem("y_out")
        pool_c = sem("pool_c"); qz_act = sem("qz_act"); gwz = sem("gwz"); dve_c = sem("dve_c")
        vaug_ok = sem("vaug_ok")
        st_ok = sem("st_ok"); lnv_ok = sem("lnv_ok"); rstd_ok = sem("rstd_ok"); xn_ok = sem("xn_ok")
        gwT_ps = sem("gwT_ps"); gwT_ok = sem("gwT_ok"); kT_ps = sem("kT_ps"); kT_ok = sem("kT_ok")
        qT_ps = sem("qT_ps"); qT_ok = sem("qT_ok"); gate_ps = sem("gate_ps"); tg_ok = sem("tg_ok")
        fmin_ok = sem("fmin_ok"); fl_ok = sem("fl_ok"); row = sem("row"); e_ok = sem("e_ok")
        spl_ok = sem("spl_ok"); ewn_ps = sem("ewn_ps"); tk_ok = sem("tk_ok")
        ekqw = sem("ekqw"); s1_ps = sem("s1_ps"); s1_ok = sem("s1_ok")
        qk_ps = sem("qk_ps"); arg_ps = sem("arg_ps"); d_ok = sem("d_ok"); ct_ok = sem("ct_ok")
        cv_ps = sem("cv_ps"); osb_ok = sem("osb_ok"); to_ps = sem("to_ps"); post = sem("post")
        h_ok = sem("h_ok"); hv_ok = sem("hv_ok"); hln_ok = sem("hln_ok"); hrs_ok = sem("hrs_ok")
        x2t = sem("x2t"); x2_ok = sem("x2_ok"); v2 = sem("v2"); v2_ok = sem("v2_ok")
        ln2_ok = sem("ln2_ok"); rs2_ok = sem("rs2_ok"); xn2_ok = sem("xn2_ok")
        xnT_ps = sem("xnT_ps"); xnT_ok = sem("xnT_ok"); lg_ps = sem("lg_ps"); rt = sem("rt")
        lm_ok = sem("lm_ok"); ex_ok = sem("ex_ok"); sc_ok = sem("sc_ok"); oh_ok = sem("oh_ok")
        cnt_ps = sem("cnt_ps"); rank_ps = sem("rank_ps"); rv_ok = sem("rv_ok"); inv_ps = sem("inv_ps")
        idx_ok = sem("idx_ok"); eb_ok = sem("eb_ok")
        xs_ps = sem("xs_ps"); xs_ok = sem("xs_ok"); h_ps = sem("h_ps"); hid_ok = sem("hid_ok")
        hT_ps = sem("hT_ps"); hT_ok = sem("hT_ok"); y_ps = sem("y_ps"); y1_ok = sem("y1_ok")
        yo_ok = sem("yo_ok")

        (C_ID0, C_ID, C_QZ, C_SEL0, C_SELT, C_SELA, C_SELS, C_SEL, C_MASK0, C_MASK, C_VZ, C_VONE,
         C_BD0, C_BD1, C_BD, C_UP0, C_UP, C_ONES, C_CI, C_PI, C_RES) = range(1, 22)

        tok_v = lambda a: a.rearrange("b (c p) d -> p (b c) d", p=P)
        block = ctx.enter_context(nc.Block())

        @block.sync
        def _(sp):
            sp.dma_start(x_sb[:, 0:4, :], tok_v(x)[:, 0:4, :]).then_inc(x_in[0], 16)
            sp.wait_ge(gwz, 1)
            for base_row, w in ((0, igw), (32, fgw)):
                sp.dma_start(gw_rows[base_row:base_row + 3 * H, :],
                             w.rearrange("(a h) d -> a h d", a=1).to_broadcast([3, H, 3 * D])).then_inc(gw_in, 16)
            sp.dma_start(gbias[:, 0:1], igb.rearrange("(a h o) -> a h o", a=1, o=1).to_broadcast([P // H, H, 1])).then_inc(gb_in, 16)
            sp.dma_start(gbias[:, 1:2], fgb.rearrange("(a h o) -> a h o", a=1, o=1).to_broadcast([P // H, H, 1])).then_inc(gb_in, 16)
            sp.wait_ge(qT_ok, 2)
            sp.wait_ge(pool_c, C_QZ)
            sp.wait_ge(qz_act, 1)
            for h in range(H):
                sp.dma_start(qbd[DH * h:DH * (h + 1), h, :], qT[DH * h:DH * (h + 1), :]).then_inc(qbd_in, 16)
            sp.dma_start(w1_sb[:, :].rearrange("p (e f) -> p e f", e=E), w1.rearrange("e d f -> d e f")).then_inc(w1_in, 16)
            sp.dma_start(w2_sb[:, :].rearrange("p (e j d) -> p e j d", e=E, j=FJ),
                         w2.rearrange("e (j p) d -> p e j d", p=P)).then_inc(w2_in, 16)
            for n in range(NT // 2):
                sp.wait_ge(sc_ok, 1)
                sp.dma_start(payload.rearrange("(n p) d -> p n d", p=P)[:, 2 * n:2 * n + 2, :],
                             pl[:, 2 * n:2 * n + 2, :]).then_inc(pl_out, 16)
            sp.wait_ge(y_out, 16 * BLOCKS)

        @block.gpsimd
        def _(pool):
            def c(ins):
                ins.then_inc(pool_c, 1)

            c(pool.memset(identf[:, :], 0.0))
            pool.wait_ge(pool_c, C_ID0)
            c(pool.affine_select(out=identf[:, :], in_=identf[:, :], compare_op=ALU.not_equal, fill=1.0,
                                 base=0, pattern=[[-1, P]], channel_multiplier=1))
            c(pool.memset(qbd[:, H // 2:H, :], 0.0))
            c(pool.memset(selt[:, :, :, :], 0.0))
            pool.wait_ge(pool_c, C_SEL0)
            c(pool.affine_select(out=selt[:, :, :, :], in_=selt[:, :, :, :], compare_op=ALU.not_equal, fill=1.0,
                                 base=0, pattern=[[-32, B], [-H, 3], [-1, H]], channel_multiplier=1))
            pool.wait_ge(pool_c, C_SELT)
            c(pool.tensor_tensor(sels[:, :, :], selt[:, :, 0, :], selt[:, :, 1, :], ALU.add))
            pool.wait_ge(pool_c, C_SELA)
            c(pool.tensor_tensor(sels[:, :, :], sels[:, :, :], selt[:, :, 2, :], ALU.add))
            pool.wait_ge(pool_c, C_SELS)
            c(pool.tensor_copy(sel[:, :, :, :].rearrange("p b h s -> p (b h) s"),
                               sels[:, :, :].rearrange("p b h -> p (b h)").unsqueeze(2).to_broadcast([P, B * H, P])))
            c(pool.memset(mask[:, :], 0.0))
            pool.wait_ge(pool_c, C_MASK0)
            c(pool.affine_select(out=mask[:, :], in_=mask[:, :], compare_op=ALU.is_ge, fill=NEG,
                                 base=0, pattern=[[0, 4], [1, P]], channel_multiplier=-1))
            c(pool.memset(vaug[:, :, :, DH + 1:VW], 0.0))
            c(pool.memset(vaug[:, :, :, DH:DH + 1], 1.0))
            pool.wait_ge(c_in, 32)
            pool.tensor_copy(vaug[:, :, :, 0:DH], c_sb[:, :, :].rearrange("p n (h d) -> p n h d", h=H)).then_inc(vaug_ok, 1)
            c(pool.memset(bd[:, :], 1.0))
            pool.wait_ge(pool_c, C_BD0)
            c(pool.affine_select(out=bd[:, :], in_=bd[:, :], compare_op=ALU.is_ge, fill=0.0,
                                 base=0, pattern=[[-DH, H], [0, VW]], channel_multiplier=1))
            pool.wait_ge(pool_c, C_BD1)
            c(pool.affine_select(out=bd[:, :], in_=bd[:, :], compare_op=ALU.is_ge, fill=0.0,
                                 base=DH - 1, pattern=[[DH, H], [0, VW]], channel_multiplier=-1))
            c(pool.memset(upper[:, :], 1.0))
            pool.wait_ge(pool_c, C_UP0)
            c(pool.affine_select(out=upper[:, :], in_=upper[:, :], compare_op=ALU.is_gt, fill=0.0,
                                 base=0, pattern=[[1, P]], channel_multiplier=-1))
            c(pool.memset(ones[:, :], 1.0))
            c(pool.iota(ci[:, :], [[1, P]], base=0, channel_multiplier=0))
            c(pool.iota(pi[:, :], [[0, 1]], base=0, channel_multiplier=1))
            c(pool.memset(reset[:, :, :], 1.0))
            pool.wait_ge(tk_ok, 1)
            for b in range(B):
                for dst, src, w in ((ek[:, b, :], c_sb[:, 2 * b, :], 0), (qw[:, b, :], xn[:, 2 * b + 1, :], 1)):
                    pool.tensor_tensor(dst.rearrange("p (h d) -> p h d", h=H), src.rearrange("p (h d) -> p h d", h=H),
                                       tk[:, w, 32 * b:32 * b + H].unsqueeze(2).to_broadcast([P, H, DH]),
                                       ALU.mult).then_inc(ekqw, 1)
            pool.wait_ge(pl_out, 16 * (NT // 2))
            pool.wait_ge(idx_ok, 2)
            AHEAD = 5

            def fetch(k):
                pool.indirect_dma_start(xg[:, k, :], None, payload, bass.IndirectOffsetOnAxis(ap=gidx[:, k:k + 1], axis=0),
                                        bounds_check=B * S - 1, oob_is_err=False).then_inc(xg_in[k], 16)

            for k in range(AHEAD):
                fetch(k)
            out_rows = out.rearrange("b s d -> (b s) d")
            for k in range(BLOCKS):
                if k + AHEAD < BLOCKS:
                    fetch(k + AHEAD)
                pool.wait_ge(yo_ok, k + 1)
                pool.indirect_dma_start(out_rows, bass.IndirectOffsetOnAxis(ap=sidx[:, k:k + 1], axis=0), yo[:, k, :], None,
                                        bounds_check=B * S - 1, oob_is_err=False).then_inc(y_out, 16)

        @block.scalar
        def _(act):
            act.dma_start(c_sb[:, 0:4, :], tok_v(ctx_in)[:, 0:4, :]).then_inc(c_in, 16)
            act.dma_start(x_sb[:, 4:8, :], tok_v(x)[:, 4:8, :]).then_inc(x_in[1], 16)
            act.dma_start(c_sb[:, 4:8, :], tok_v(ctx_in)[:, 4:8, :]).then_inc(c_in, 16)
            act.dma_start(gate[:, 0:1], g_x.rearrange("(a o) -> a o", o=1).to_broadcast([P, 1])).then_inc(gate_in, 16)
            act.dma_start(gate[:, 1:2], g_f.rearrange("(a o) -> a o", o=1).to_broadcast([P, 1])).then_inc(gate_in, 16)
            act.dma_start(lnsr[:, :], lns.rearrange("(a d) -> a d", a=1).to_broadcast([P, D])).then_inc(lns_in, 16)
            act.dma_start(sw_sb[:, :], sw).then_inc(sw_in, 16)
            act.dma_start(sbr[:, :], sb_.rearrange("(a d) -> a d", a=1).to_broadcast([P, E])).then_inc(sw_in, 16)
            act.dma_start(b1_rows[:, :], b1.rearrange("e (j p) -> (e j) p", p=P)).then_inc(b_in, 16)
            act.dma_start(b2r[:, :], b2.rearrange("(a e) d -> a (e d)", a=1).to_broadcast([P, E * D])).then_inc(b_in, 16)
            act.memzero(qbd[:, 0:H // 2, :]).then_inc(qz_act, 1)
            act.wait_ge(gate_in, 32)
            act.activation(tg[:, :], gate[:, :], ACT.Tanh).then_inc(tg_ok, 1)
            act.wait_ge(st_ok, 2 * NT)
            act.activation(lnv[:, :], mv[:, :, 1], ACT.Ln, bias=DH * LN_EPS, scale=float(DH)).then_inc(lnv_ok, 1)
            act.wait_ge(lnv_ok, 1)
            act.activation(rstd[:, :], lnv[:, :], ACT.Exp, scale=-0.5).then_inc(rstd_ok, 1)
            for i in range(2):
                act.wait_ge(kT_ps, i + 1)
                act.activation(kT[:, 512 * i:512 * (i + 1)], bank[i][:, :], ACT.Copy).then_inc(kT_ok, 1)
            act.wait_ge(gate_ps, 1)
            act.wait_ge(gb_in, 32)
            act.activation(fabs[:, :], bank[4][:, 0:S], ACT.Abs, bias=gbias[:, 1:2]).then_inc(fl_ok, 1)
            act.wait_ge(fl_ok, 1)
            act.activation(fexp[:, :], fabs[:, :], ACT.Exp, scale=-1.0).then_inc(fl_ok, 1)
            act.wait_ge(fl_ok, 2)
            act.activation(fln[:, :], fexp[:, :], ACT.Ln, bias=1.0).then_inc(fl_ok, 1)
            act.wait_ge(row, 4)
            act.activation(ewn[:, 0:P], am[:, 0, 0:P], ACT.Exp, bias=am[:, 1, P - 1:P]).then_inc(e_ok, 1)
            act.wait_ge(row, 5)
            act.activation(ewn[:, P:2 * P], am[:, 1, P:S], ACT.Exp, bias=m1[:, :]).then_inc(e_ok, 1)
            act.wait_ge(row, 6)
            act.activation(ewn[:, 2 * P:4 * P], nm[:, :], ACT.Exp).then_inc(e_ok, 1)

            def decay(u):
                act.wait_ge(arg_ps, u + 1)
                if u >= 2:
                    act.wait_ge(ct_ok, u - 1)
                act.activation(dmat[:, u % 2, :], bank[2 + u % 2][:, :], ACT.Exp).then_inc(d_ok, 1)

            def take_out(n):
                act.wait_ge(cv_ps, G * (n + 1))
                if n >= 2:
                    act.wait_ge(to_ps, n - 1)
                act.activation(osb[:, n % 2, :], bank[4 + n % 2][:, 0:2 * P], ACT.Copy).then_inc(osb_ok, 1)

            def rstd_h(b):
                act.wait_ge(hv_ok, 2 * (b + 1))
                act.activation(hln[:, 2 * b:2 * b + 2], hmv[:, 2 * b:2 * b + 2, 1], ACT.Ln, bias=LN_EPS).then_inc(hln_ok, 1)
                act.wait_ge(hln_ok, b + 1)
                act.activation(hrs[:, 2 * b:2 * b + 2], hln[:, 2 * b:2 * b + 2], ACT.Exp, scale=-0.5).then_inc(hrs_ok, 1)

            def rstd_2(b):
                act.wait_ge(v2_ok, 2 * (b + 1))
                act.activation(ln2[:, 2 * b:2 * b + 2], mv2[:, 2 * b:2 * b + 2, 1], ACT.Ln, bias=LN_EPS).then_inc(ln2_ok, 1)
                act.wait_ge(ln2_ok, b + 1)
                act.activation(rs2[:, 2 * b:2 * b + 2], ln2[:, 2 * b:2 * b + 2], ACT.Exp, scale=-0.5).then_inc(rs2_ok, 1)

            decay(0)
            decay(1)
            for u in range(U + 6):
                if u + 2 < U:
                    decay(u + 2)
                if u < U and u % G == G - 1:
                    take_out(u // G)
                if u >= 5 and (u - 5) % 4 == 0 and (u - 5) // 4 < B:
                    rstd_h((u - 5) // 4)
                if u >= 7 and (u - 7) % 4 == 0 and (u - 7) // 4 < B:
                    rstd_2((u - 7) // 4)
            act.wait_ge(lm_ok, 1)
            act.activation(ex[:, :, :], lm[:, :, :], ACT.Exp).then_inc(ex_ok, 1)
            act.wait_ge(eb_ok, 1)
            for k in range(BLOCKS):
                e = act.value_load(ebi[0:1, k:k + 1], min_val=0, max_val=E - 1)
                act.wait_ge(hT_ps, k + 1)
                if k >= 2:
                    act.wait_ge(y_ps, k - 1)
                for j in range(FJ):
                    act.activation(hT[:, k % 2, j, :], bank[2 + k % 2][:, P * j:P * (j + 1)], ACT.Gelu_apprx_tanh,
                                   bias=b1T[:, bass.ds(e * FJ + j, 1)]).then_inc(hT_ok, 1)

        @block.vector
        def _(dve):
            dve.memset(gw_rows[:, :], 0.0).then_inc(gwz, 1)
            for n in range(NT):
                if n % 4 == 0:
                    dve.wait_ge(x_in[n // 4], 16)
                dve.bn_stats(st[:, n, :], x_sb[:, n, :]).then_inc(st_ok, 1)
            dve.wait_ge(st_ok, NT)
            for n in range(NT):
                dve.bn_aggr(mv[:, n, :], st[:, n, :]).then_inc(st_ok, 1)
            dve.wait_ge(rstd_ok, 1)
            for n in range(NT):
                dve.tensor_scalar(xn[:, n, :], x_sb[:, n, :], mv[:, n, 0:1], rstd[:, n:n + 1],
                                  ALU.subtract, ALU.mult).then_inc(xn_ok, 1)
            dve.wait_ge(gwT_ps, 1)
            dve.tensor_scalar(gwT[:, 0, :], bank[7][:, 0:64], 4.0, None, ALU.mult).then_inc(gwT_ok, 1)
            dve.tensor_copy(gwT[:, 1, :], bank[7][:, 64:128]).then_inc(gwT_ok, 1)
            dve.wait_ge(gwT_ok, 2)
            dve.tensor_tensor(gwT[:, 1, :], gwT[:, 1, :], bank[7][:, 128:192], ALU.add).then_inc(gwT_ok, 1)
            dve.tensor_copy(b1T[:, :], bank[7][:, 192:192 + E * FJ]).then_inc(gwT_ok, 1)
            for i in range(2):
                dve.wait_ge(qT_ps, i + 1)
                dve.tensor_copy(qT[:, 512 * i:512 * (i + 1)], bank[2 + i][:, :]).then_inc(qT_ok, 1)
            dve.wait_ge(pool_c, C_RES)
            dve.tensor_scalar(jrow[:, :], pi[:, :], 24, None, ALU.bitwise_and).then_inc(dve_c, 1)
            dve.wait_ge(dve_c, 1)
            dve.tensor_scalar(negk[:, 0:1], jrow[:, :], 8.0, -1.0, ALU.is_ge, ALU.mult).then_inc(dve_c, 1)
            dve.tensor_scalar(negk[:, 1:2], jrow[:, :], 16.0, -1.0, ALU.is_ge, ALU.mult).then_inc(dve_c, 1)
            dve.tensor_copy(identb[:, :], identf[:, :]).then_inc(dve_c, 1)
            dve.wait_ge(gate_ps, 2)
            dve.wait_ge(gb_in, 32)
            dve.wait_ge(fl_ok, 1)
            dve.tensor_scalar(fmin[:, :], bank[4][:, 0:S], gbias[:, 1:2], 0.0, ALU.add, ALU.min).then_inc(fmin_ok, 1)
            dve.wait_ge(fmin_ok, 1)
            dve.wait_ge(fl_ok, 3)
            dve.tensor_tensor_scan(cs[:, :], fmin[:, :], fln[:, :], 0.0, ALU.add, ALU.subtract).then_inc(row, 1)
            dve.wait_ge(row, 1)
            dve.scalar_tensor_tensor(out=am[:, 0, :], in0=bank[5][:, 0:S], scalar=gbias[:, 0:1], in1=cs[:, :],
                                     op0=ALU.add, op1=ALU.subtract).then_inc(row, 1)
            dve.wait_ge(row, 2)
            dve.tensor_scalar(nega[:, :], am[:, 0, :], -1.0, None, ALU.mult).then_inc(row, 1)
            dve.wait_ge(row, 3)
            dve.tensor_tensor_scan(am[:, 1, :], nega[:, :], nega[:, :], 3e38, ALU.min, ALU.min).then_inc(row, 1)
            dve.wait_ge(row, 4)
            dve.tensor_scalar(m1[:, :], am[:, 1, P - 1:P], -1.0, None, ALU.mult).then_inc(row, 1)
            dve.tensor_tensor(nm[:, :], am[:, 1, :], cs[:, :], ALU.subtract).then_inc(row, 1)
            amf = am[:, :, :].rearrange("p a s -> p (a s)")
            dve.tensor_copy(s0[:, :], amf).then_inc(row, 1)
            dve.wait_ge(row, 7)
            dve.wait_ge(dve_c, 3)
            dve.scalar_tensor_tensor(out=r1[:, :], in0=s0[:, :], scalar=negk[:, 0:1], in1=amf,
                                     op0=ALU.mult, op1=ALU.add).then_inc(row, 1)
            dve.wait_ge(row, 8)
            dve.tensor_copy(s1[:, :], r1[:, :]).then_inc(row, 1)
            dve.wait_ge(row, 9)
            dve.scalar_tensor_tensor(out=spl[:, :, :].rearrange("p a s -> p (a s)"), in0=s1[:, :], scalar=negk[:, 1:2],
                                     in1=r1[:, :], op0=ALU.mult, op1=ALU.add).then_inc(spl_ok, 1)
            dve.wait_ge(ewn_ps, 1)
            dve.tensor_copy(tk[:, :, :].rearrange("p a s -> p (a s)"), bank[6][:, :]).then_inc(tk_ok, 1)
            dve.wait_ge(tg_ok, 1)
            dve.wait_ge(lns_in, 16)
            dve.tensor_scalar(g1r[:, :], lnsr[:, :], tg[:, 0:1], None, ALU.mult).then_inc(dve_c, 1)
            dve.tensor_copy(cf[:, :], ci[:, :]).then_inc(dve_c, 1)
            dve.tensor_copy(cv[:, :, 0], pi[:, :].to_broadcast([P, NT])).then_inc(dve_c, 1)
            dve.memset(reset[:, :, 0:1], 0.0).then_inc(dve_c, 1)
            dve.memset(cv[:, :, 2], 1.0).then_inc(dve_c, 1)
            dve.wait_ge(dve_c, 9)
            dve.tensor_copy(cv[:, :, 1], cf[:, 0:NT]).then_inc(dve_c, 1)
            dve.tensor_scalar(c128[:, :], cf[:, 0:16], float(P), None, ALU.mult).then_inc(dve_c, 1)
            dve.tensor_scalar(dec[:, :], cf[:, 0:E], -1.0, float(E), ALU.mult, ALU.add).then_inc(dve_c, 1)
            dve.memset(pl[:, :, 2 * D:PLW], 0.0).then_inc(dve_c, 1)

            def weigh(u):
                dve.wait_ge(qk_ps, u + 1)
                dve.wait_ge(d_ok, u + 1)
                if u >= 2:
                    dve.wait_ge(cv_ps, u - 1)
                dve.tensor_tensor(ct[:, u % 2, :], bank[u % 2][:, :], dmat[:, u % 2, :], ALU.mult).then_inc(ct_ok, 1)

            def state(b):
                dve.wait_ge(s1_ps, b + 1)
                if b >= 2:
                    dve.wait_ge(cv_ps, 4 * (b - 2) + 4)
                dve.tensor_tensor(s1bd[:, b % 2, :], bank[6][:, 0:H * VW], bd[:, :], ALU.mult).then_inc(s1_ok, 1)
                dve.tensor_copy(qwT[:, b % 2, :], bank[6][:, 256:256 + P]).then_inc(s1_ok, 1)

            def normalise(n):
                b, c = n // 2, n % 2
                to = bank[6 + n % 2][:, 0:H * VW].rearrange("p (h w) -> p h w", h=H)
                dve.wait_ge(to_ps, n + 1)
                i = 4 * n
                dve.tensor_tensor(nrm[:, 0, :], to[:, :, DH], tk[:, 2 + c, 32 * b:32 * b + H], ALU.max).then_inc(post, 1)
                dve.wait_ge(post, i + 1)
                dve.scalar_tensor_tensor(out=nrm[:, 1, :], in0=to[:, :, DH], scalar=-1.0, in1=nrm[:, 0, :],
                                         op0=ALU.mult, op1=ALU.max).then_inc(post, 1)
                dve.wait_ge(post, i + 2)
                dve.tensor_scalar(nrm[:, 2, :], nrm[:, 1, :], EPS, None, ALU.add).then_inc(post, 1)
                dve.wait_ge(post, i + 3)
                dve.reciprocal(nrm[:, 3, :], nrm[:, 2, :]).then_inc(post, 1)
                dve.wait_ge(post, i + 4)
                dve.tensor_tensor(hh[:, n, :].rearrange("p (h d) -> p h d", h=H), to[:, :, 0:DH],
                                  nrm[:, 3, :].unsqueeze(2).to_broadcast([P, H, DH]), ALU.mult).then_inc(h_ok, 1)
                dve.wait_ge(h_ok, 2 * n + 1)
                dve.bn_stats(hst[:, n, :], hh[:, n, :]).then_inc(h_ok, 1)
                dve.wait_ge(h_ok, 2 * n + 2)
                dve.bn_aggr(hmv[:, n, :], hst[:, n, :]).then_inc(hv_ok, 1)

            def residual(b):
                dve.wait_ge(hrs_ok, b + 1)
                dve.wait_ge(dve_c, 5)
                if b >= 1:
                    dve.wait_ge(x2_ok, 2 * b)
                for i in range(2):
                    n = 2 * b + i
                    dve.scalar_tensor_tensor(out=tmp[:, i, :], in0=hh[:, n, :], scalar=hmv[:, n, 0:1], in1=g1r[:, :],
                                             op0=ALU.subtract, op1=ALU.mult).then_inc(x2t, 1)
                for i in range(2):
                    n = 2 * b + i
                    dve.wait_ge(x2t, n + 1)
                    dve.scalar_tensor_tensor(out=pl[:, n, 0:D], in0=tmp[:, i, :], scalar=hrs[:, n:n + 1], in1=x_sb[:, n, :],
                                             op0=ALU.mult, op1=ALU.add).then_inc(x2_ok, 1)
                for i in range(2):
                    n = 2 * b + i
                    dve.wait_ge(x2_ok, n + 1)
                    dve.bn_stats(st2[:, n, :], pl[:, n, 0:D]).then_inc(v2, 1)
                for i in range(2):
                    n = 2 * b + i
                    dve.wait_ge(v2, n + 1)
                    dve.bn_aggr(mv2[:, n, :], st2[:, n, :]).then_inc(v2_ok, 1)

            def norm_2(b):
                dve.wait_ge(rs2_ok, b + 1)
                for n in (2 * b, 2 * b + 1):
                    dve.tensor_scalar(pl[:, n, D:2 * D], pl[:, n, 0:D], mv2[:, n, 0:1], rs2[:, n:n + 1],
                                      ALU.subtract, ALU.mult).then_inc(xn2_ok, 1)

            for u in range(U + 6):
                if u < U:
                    weigh(u)
                if u < U and u % 4 == 1:
                    state(u // 4)
                if u >= 3 and u % 2 == 1 and (u - 3) // 2 < NT:
                    normalise((u - 3) // 2)
                if u >= 6 and (u - 6) % 4 == 0 and (u - 6) // 4 < B:
                    residual((u - 6) // 4)
                if u >= 8 and (u - 8) % 4 == 0 and (u - 8) // 4 < B:
                    norm_2((u - 8) // 4)
            for i in range(2):
                dve.wait_ge(xnT_ps, i + 1)
                dve.tensor_copy(xnT[:, 512 * i:512 * (i + 1)], bank[i][:, :]).then_inc(xnT_ok, 1)
            n_rt = [0]

            def link(ins):
                n_rt[0] += 1
                ins.then_inc(rt, 1)
                dve.wait_ge(rt, n_rt[0])

            rep = lambda a, k: a.unsqueeze(2).to_broadcast([P, a.shape[1], k])
            per = lambda a, k: a.unsqueeze(1).to_broadcast([P, k, a.shape[1]])
            dve.wait_ge(sw_in, 32)
            dve.wait_ge(lg_ps, 1)
            link(dve.tensor_tensor(lg[:, :, :], bank[2][:, 0:NT * E].rearrange("p (n e) -> p n e", n=NT),
                                   per(sbr[:, :], NT), ALU.add))
            link(dve.reduce_max(mx[:, :], lg[:, :, :], X))
            dve.tensor_tensor(lm[:, :, :], lg[:, :, :], rep(mx[:, :], E), ALU.subtract).then_inc(lm_ok, 1)
            dve.wait_ge(lm_ok, 1)
            dve.wait_ge(dve_c, 13)
            link(dve.tensor_scalar(enc[:, :, :], lm[:, :, :], 0.0, None, ALU.is_ge))
            link(dve.tensor_tensor(enc[:, :, :], enc[:, :, :], per(dec[:, :], NT), ALU.mult))
            link(dve.reduce_max(first[:, :], enc[:, :, :], X))
            dve.tensor_tensor(oh[:, :, :], per(dec[:, :], NT), rep(first[:, :], E), ALU.is_equal).then_inc(oh_ok, 1)
            dve.wait_ge(ex_ok, 1)
            link(dve.reduce_sum(sm[:, :], ex[:, :, :], X))
            link(dve.reciprocal(rsm[:, :], sm[:, :]))
            dve.tensor_scalar(pl[:, :, 2 * D:2 * D + 1], rsm[:, :].unsqueeze(2), tg[:, 1:2], None, ALU.mult).then_inc(sc_ok, 1)
            dve.wait_ge(cnt_ps, 1)
            link(dve.tensor_copy(cnt[:, :, :], bank[3][:, 0:NT * E].rearrange("p (n e) -> p e n", n=NT)))
            link(dve.tensor_tensor_scan(incl[:, :, :].rearrange("p e n -> p (e n)"), reset[:, :, :].rearrange("p e n -> p (e n)"),
                                        cnt[:, :, :].rearrange("p e n -> p (e n)"), 0.0, ALU.mult, ALU.add))
            link(dve.tensor_tensor(gtk[:, :, :], rep(incl[:, :, NT - 1], 8), per(c128[:, 0:8], E), ALU.is_gt))
            link(dve.reduce_sum(nb[:, :], gtk[:, :, :], X))
            link(dve.tensor_tensor_scan(bend[:, :], nb[:, :], nb[:, :], 0.0, ALU.add, ALU.bypass))
            link(dve.tensor_tensor(bst[:, :], bend[:, :], nb[:, :], ALU.subtract))
            link(dve.scalar_tensor_tensor(out=base[:, :, :], in0=rep(bst[:, :], NT), scalar=float(P), in1=incl[:, :, :],
                                          op0=ALU.mult, op1=ALU.add))
            link(dve.tensor_tensor(base[:, :, :], base[:, :, :], cnt[:, :, :], ALU.subtract))
            dve.wait_ge(rank_ps, 1)
            link(dve.tensor_tensor(t1[:, :, :], bank[4][:, 0:NT * E].rearrange("p (n e) -> p n e", n=NT),
                                   base[:, :, :].rearrange("p e n -> p n e"), ALU.add))
            link(dve.tensor_tensor(t2[:, :, :], t1[:, :, :], oh[:, :, :], ALU.mult))
            link(dve.reduce_sum(slot[:, :], t2[:, :, :], X))
            link(dve.tensor_tensor(gek[:, :, 0:15], rep(slot[:, :], 15), per(c128[:, 1:16], NT), ALU.is_ge))
            link(dve.reduce_sum(blk[:, :], gek[:, :, 0:15], X))
            link(dve.scalar_tensor_tensor(out=off[:, :], in0=blk[:, :], scalar=-float(P), in1=slot[:, :], op0=ALU.mult, op1=ALU.add))
            link(dve.tensor_tensor(ohb[:, :, :], rep(blk[:, :], 16), per(cf[:, 0:16], NT), ALU.is_equal))
            dve.tensor_tensor(ohoff[:, :, :], rep(off[:, :], P), per(cf[:, :], NT), ALU.is_equal).then_inc(rv_ok, 1)
            for c in range(3):
                dve.tensor_tensor(rv[:, :, c, :], ohb[:, :, :], rep(cv[:, :, c], 16), ALU.mult).then_inc(rv_ok, 1)
            link(dve.tensor_tensor(ebc[:, :, :], rep(cf[:, 0:16], E), per(bend[:, :], 16), ALU.is_ge))
            link(dve.reduce_sum(ebf[:, :], ebc[:, :, :], X))
            dve.tensor_scalar(ebi[:, :], ebf[:, :], float(E - 1), None, ALU.min).then_inc(eb_ok, 1)
            dve.wait_ge(inv_ps, 1)
            link(dve.tensor_copy(inv[:, :, :], bank[5][:, 0:48].rearrange("p (c k) -> p c k", c=3)))
            link(dve.scalar_tensor_tensor(out=tok[:, :], in0=inv[:, 1, :], scalar=float(P), in1=inv[:, 0, :], op0=ALU.mult, op1=ALU.add))
            dve.tensor_copy(gidx[:, :], tok[:, :]).then_inc(idx_ok, 1)
            link(dve.tensor_scalar(pad[:, :], inv[:, 2, :], -4096.0, 4096.0, ALU.mult, ALU.add))
            dve.tensor_tensor(sidx[:, :], tok[:, :], pad[:, :], ALU.add).then_inc(idx_ok, 1)
            dve.wait_ge(eb_ok, 1)
            dve.wait_ge(b_in, 32)

            def take_rows(k):
                dve.wait_ge(xs_ps, k + 1)
                dve.tensor_copy(xsT[:, k % 2, :], bank[6 + k % 2][:, 0:P]).then_inc(xs_ok, 1)

            take_rows(0)
            for k in range(BLOCKS + 2):
                if k + 1 < BLOCKS:
                    take_rows(k + 1)
                if k < BLOCKS:
                    dve.wait_ge(h_ps, k + 1)
                    if k >= 2:
                        dve.wait_ge(hT_ps, k - 1)
                    dve.tensor_copy(hid[:, k % 2, :], bank[k % 2][:, :]).then_inc(hid_ok, 1)
                if k >= 2:
                    m = k - 2
                    e = dve.value_load(ebi[0:1, m:m + 1], min_val=0, max_val=E - 1)
                    dve.wait_ge(y_ps, m + 1)
                    dve.tensor_tensor(y1[:, m % 2, :], bank[4 + m % 2][:, 0:D], b2r[:, bass.ds(e * D, D)], ALU.add).then_inc(y1_ok, 1)
                    dve.wait_ge(y1_ok, m + 1)
                    dve.scalar_tensor_tensor(out=yo[:, m, :], in0=y1[:, m % 2, :], scalar=xg[:, m, 2 * D:2 * D + 1],
                                             in1=xg[:, m, 0:D], op0=ALU.mult, op1=ALU.add).then_inc(yo_ok, 1)

        @block.tensor
        def _(pe):
            pe.wait_ge(pool_c, C_ID)
            pe.wait_ge(gw_in, 32)
            for i in range(3):
                pe.transpose(bank[7][:, 64 * i:64 * (i + 1)], gw_rows[:, D * i:D * (i + 1)], identf[0:64, 0:64])
            pe.wait_ge(b_in, 32)
            pe.transpose(bank[7][:, 192:192 + E * FJ], b1_rows[:, :], identf[0:E * FJ, 0:E * FJ]).then_inc(gwT_ps, 1)
            pe.wait_ge(c_in, 32)
            for n in range(NT):
                t = pe.transpose(bank[n // 4][:, P * (n % 4):P * (n % 4 + 1)], c_sb[:, n, :], identf[:, :])
                if n % 4 == 3:
                    t.then_inc(kT_ps, 1)
            for n in range(NT):
                pe.wait_ge(xn_ok, n + 1)
                t = pe.transpose(bank[2 + n // 4][:, P * (n % 4):P * (n % 4 + 1)], xn[:, n, :], identf[:, :])
                if n % 4 == 3:
                    t.then_inc(qT_ps, 1)
            pe.wait_ge(gwT_ok, 4)
            pe.wait_ge(qT_ok, 2)
            pe.wait_ge(kT_ok, 2)
            for to, col in ((4, 32), (5, 0)):
                for part, src in ((0, qT), (1, kT)):
                    for b in range(B):
                        t = pe.matmul(bank[to][32 * b:32 * b + 32, 0:S], gwT[:, part, col:col + 32],
                                      src[:, S * b:S * (b + 1)], start=(part == 0), stop=(part == 1), skip_group_check=True)
                t.then_inc(gate_ps, 1)

            def scores(u):
                n, g = u // G, u % G
                if u >= 2:
                    pe.wait_ge(ct_ok, u - 1)
                pe.matmul(bank[u % 2][:, :], kT[:, P * n:P * (n + 1)], qbd[:, 4 * g:4 * g + 4, P * n:P * (n + 1)],
                          start=True, stop=True).then_inc(qk_ps, 1)

            def exponents(u):
                n, g = u // G, u % G
                b, c = n // 2, n % 2
                if u >= 2:
                    pe.wait_ge(d_ok, u - 1)
                to = bank[2 + u % 2]
                pe.matmul(to[:, :], identb[:, :], mask[:, :], start=True, stop=False, skip_group_check=True)
                pe.matmul(to[:, :], spl[:, 0, P * c:P * (c + 1)], sel[:, b, 4 * g:4 * g + 4, :],
                          start=False, stop=False, skip_group_check=True)
                for i in range(4):
                    t = pe.matmul(to[:, P * i:P * (i + 1)], sel[:, b, 4 * g + i, :], spl[:, 1, P * c:P * (c + 1)],
                                  start=False, stop=(i == 3), skip_group_check=True)
                t.then_inc(arg_ps, 1)

            def values(u):
                n, g = u // G, u % G
                b, c = n // 2, n % 2
                pe.wait_ge(ct_ok, u + 1)
                if g == 0 and n >= 2:
                    pe.wait_ge(osb_ok, n - 1)
                to = bank[4 + n % 2]
                if c == 1:
                    pe.wait_ge(s1_ok, 2 * b + 2)
                    pe.matmul(to[:, P * g:P * (g + 1)], s1bd[:, b % 2, P * g:P * (g + 1)], qwT[:, b % 2, :],
                              start=True, stop=False, skip_group_check=True)
                for i in range(4):
                    t = pe.matmul(to[32 * i:32 * i + DH + 1, P * g:P * (g + 1)], vaug[:, n, 4 * g + i, 0:DH + 1],
                                  ct[:, u % 2, P * i:P * (i + 1)], start=(c == 0), stop=True, skip_group_check=True)
                t.then_inc(cv_ps, 1)

            def turn_back(n):
                pe.wait_ge(osb_ok, n + 1)
                if n >= 2:
                    pe.wait_ge(h_ok, 2 * (n - 2) + 1)
                if n >= 2 and n % 2 == 0:
                    pe.wait_ge(s1_ok, 2 * (n // 2) + 2)
                for g in range(G):
                    t = pe.transpose(bank[6 + n % 2][:, P * g:P * (g + 1)], osb[:, n % 2, P * g:P * (g + 1)], identf[:, :])
                t.then_inc(to_ps, 1)

            def state(b):
                pe.wait_ge(ekqw, 2 * b + 2)
                pe.wait_ge(vaug_ok, 1)
                if b >= 1:
                    pe.wait_ge(h_ok, 2 * (2 * b - 2) + 1)
                pe.matmul(bank[6][:, 0:H * VW], ek[:, b, :], vaug[:, 2 * b, :, :], start=True, stop=True)
                pe.transpose(bank[6][:, 256:256 + P], qw[:, b, :], identf[:, :]).then_inc(s1_ps, 1)

            pe.wait_ge(qbd_in, 16 * H)
            scores(0)
            scores(1)
            pe.wait_ge(e_ok, 3)
            for i in range(4):
                t = pe.transpose(bank[6][:, P * i:P * (i + 1)], ewn[:, P * i:P * (i + 1)], identf[:, :])
            t.then_inc(ewn_ps, 1)
            pe.wait_ge(spl_ok, 1)
            pe.wait_ge(dve_c, 4)
            exponents(0)
            exponents(1)
            pe.wait_ge(tk_ok, 1)
            for u in range(U):
                if u + 2 < U:
                    exponents(u + 2)
                    scores(u + 2)
                values(u)
                if u % 4 == 0:
                    state(u // 4)
                if u >= 2 and u % 2 == 0:
                    turn_back(u // 2 - 1)
            turn_back(NT - 1)
            for n in range(NT):
                pe.wait_ge(xn2_ok, n + 1)
                t = pe.transpose(bank[n // 4][:, P * (n % 4):P * (n % 4 + 1)], pl[:, n, D:2 * D], identf[:, :])
                if n % 4 == 3:
                    t.then_inc(xnT_ps, 1)
            pe.wait_ge(sw_in, 32)
            for n in range(NT):
                if n % 4 == 0:
                    pe.wait_ge(xnT_ok, n // 4 + 1)
                t = pe.matmul(bank[2][:, E * n:E * (n + 1)], xnT[:, P * n:P * (n + 1)], sw_sb[:, :], start=True, stop=True)
            t.then_inc(lg_ps, 1)
            pe.wait_ge(oh_ok, 1)
            ohf = oh[:, :, :].rearrange("p n e -> p (n e)")
            pe.matmul(bank[3][:, 0:NT * E], ones[:, :], ohf, start=True, stop=True).then_inc(cnt_ps, 1)
            pe.matmul(bank[4][:, 0:NT * E], upper[:, :], ohf, start=True, stop=True).then_inc(rank_ps, 1)
            pe.wait_ge(rv_ok, 4)
            for n in range(NT):
                t = pe.matmul(bank[5][:, 0:48], ohoff[:, n, :], rv[:, n, :, :].rearrange("p c k -> p (c k)"),
                              start=(n == 0), stop=(n == NT - 1))
            t.then_inc(inv_ps, 1)

            def rows(k):
                pe.wait_ge(xg_in[k], 16)
                if k >= 2:
                    pe.wait_ge(xs_ok, k - 1)
                pe.transpose(bank[6 + k % 2][:, 0:P], xg[:, k, D:2 * D], identf[:, :]).then_inc(xs_ps, 1)

            def up(k):
                e = pe.value_load(ebi[0:1, k:k + 1], min_val=0, max_val=E - 1)
                pe.wait_ge(xs_ok, k + 1)
                if k >= 2:
                    pe.wait_ge(hid_ok, k - 1)
                pe.matmul(bank[k % 2][:, :], xsT[:, k % 2, :], w1_sb[:, bass.ds(e * F, F)], start=True, stop=True).then_inc(h_ps, 1)

            def turn(k):
                pe.wait_ge(hid_ok, k + 1)
                if k >= 2:
                    pe.wait_ge(hT_ok, FJ * (k - 1))
                for j in range(FJ):
                    t = pe.transpose(bank[2 + k % 2][:, P * j:P * (j + 1)], hid[:, k % 2, P * j:P * (j + 1)], identf[:, :])
                t.then_inc(hT_ps, 1)

            def down(k):
                e = pe.value_load(ebi[0:1, k:k + 1], min_val=0, max_val=E - 1)
                pe.wait_ge(hT_ok, FJ * (k + 1))
                if k >= 2:
                    pe.wait_ge(yo_ok, k - 1)
                for j in range(FJ):
                    t = pe.matmul(bank[4 + k % 2][:, 0:D], hT[:, k % 2, j, :], w2_sb[:, bass.ds(e * F + D * j, D)],
                                  start=(j == 0), stop=(j == FJ - 1))
                t.then_inc(y_ps, 1)

            pe.wait_ge(eb_ok, 1)
            pe.wait_ge(w1_in, 16)
            pe.wait_ge(w2_in, 16)
            rows(0)
            for k in range(BLOCKS + 2):
                if k + 1 < BLOCKS:
                    rows(k + 1)
                if k < BLOCKS:
                    up(k)
                if 1 <= k <= BLOCKS:
                    turn(k - 1)
                if k >= 2:
                    down(k - 2)


_INS = ['x', 'ctx_1024', 'g_xattn', 'g_ffn', 'L0_xattn_igate_w', 'L0_xattn_igate_b', 'L0_xattn_fgate_w',
        'L0_xattn_fgate_b', 'L0_xattn_ln_scale', 'L0_ffn_switch_w', 'L0_ffn_switch_b', 'L0_ffn_w1', 'L0_ffn_b1',
        'L0_ffn_w2', 'L0_ffn_b2']
_OUTS = [((4, 256, 128), 'float32')]


def kernel(**inputs):
    import numpy as _np
    import concourse.bacc as _bacc
    from concourse import mybir as _mybir
    from concourse.bass_utils import run_bass_kernel_spmd as _run

    nc = _bacc.Bacc("TRN2", target_bir_lowering=False, num_devices=1)
    arrays, args = {}, []
    for name in _INS:
        a = _np.ascontiguousarray(inputs[name])
        arrays[f"in_{name}_dram"] = a
        args.append(nc.dram_tensor(f"in_{name}_dram", a.shape, _mybir.dt.from_np(a.dtype), kind="ExternalInput").ap())
    for i, (shape, dtype) in enumerate(_OUTS):
        dt = _mybir.dt.from_np(_np.dtype(dtype))
        args.append(nc.dram_tensor(f"out_{i}_dram", shape, dt, kind="ExternalOutput").ap())
    gated_block(nc, *args)
    r = _run(nc, [arrays], core_ids=[0])
    got = tuple(r.results[0][f"out_{i}_dram"] for i in range(len(_OUTS)))
    return got[0]
```

```python
from contextlib import ExitStack

import concourse.bass as bass
from concourse import mybir
from concourse.alu_op_type import AluOpType as ALU

ACT = mybir.ActivationFunctionType
F32 = mybir.dt.float32
BF16 = mybir.dt.bfloat16
I32 = mybir.dt.int32
X = mybir.AxisListType.X

P = 128
NEG = -1e30
LN_EPS = 1e-5
EPS = 1e-6


def gated_block(nc, x, ctx_in, g_x, g_f, igw, igb, fgw, fgb, lns, sw, sb_, w1, b1, w2, b2, out):
    B, S, D = x.shape
    H = igw.shape[0]
    DH = D // H
    E, _, F = w1.shape
    NT = B * S // P
    G = H // 4
    U = NT * G
    UB = 2 * G
    FJ = F // P
    VW = 32
    Q = NT + E - 1
    WBUF = 4
    assert D == P and S == 2 * P and DH == 16 and FJ == 4 and NT == 2 * B and UB == 4 and E == H

    ctx = ExitStack()
    with ctx:
        def sb(name, shape, dt=F32):
            return ctx.enter_context(nc.sbuf_tensor(name, shape, dt))

        def sem(name):
            return ctx.enter_context(nc.semaphore(name))

        bank = [ctx.enter_context(nc.psum_tensor(f"bank{i}", [P, 512], F32)) for i in range(8)]
        payload = nc.dram_tensor("payload", (B * S, 2 * D), F32, kind="Internal").ap()

        x_sb = sb("x_sb", [P, NT, D])
        c_sb = sb("c_sb", [P, NT, D])
        gw_rows = sb("gw_rows", [64, 3 * D])
        gbias = sb("gbias", [P, 2])
        gate = sb("gate", [P, 2])
        lnsr = sb("lnsr", [P, D])
        sw_sb = sb("sw_sb", [P, E])
        sbr = sb("sbr", [P, E])
        b1_rows = sb("b1_rows", [E * FJ, P])
        b2_rows = sb("b2_rows", [P, D])
        w2_sb = sb("w2_sb", [P, E * F])
        identf = sb("identf", [P, P])
        identb = sb("identb", [P, P], BF16)
        mask = sb("mask", [P, 512], BF16)
        selt = sb("selt", [P, B, 3, H])
        sels = sb("sels", [P, B, H])
        sel = sb("sel", [P, B, H, P], BF16)
        bd = sb("bd", [P, H * VW])
        upper = sb("upper", [P, P], BF16)
        ones = sb("ones", [P, P], BF16)
        ci = sb("ci", [P, P], I32)
        cf = sb("cf", [P, P])
        c128 = sb("c128", [P, NT])
        pi = sb("pi", [P, 1], I32)
        pf = sb("pf", [P, 1])
        dec = sb("dec", [P, E])
        zero8 = sb("zero8", [P, E])
        jrow = sb("jrow", [P, 1], I32)
        b2s = sb("b2s", [P, 2, D], BF16)
        b2t = sb("b2t", [P, D])
        b2p = sb("b2p", [P, D], BF16)
        kj = sb("kj", [P, 3])
        tg = sb("tg", [P, 2])
        g1r = sb("g1r", [P, D])
        st = sb("st", [P, NT, 6])
        mv = sb("mv", [P, NT, 2])
        lnv = sb("lnv", [P, NT])
        rstd = sb("rstd", [P, NT])
        xn = sb("xn", [P, NT, D])
        gwT = sb("gwT", [P, 2, 64])
        b1T = sb("b1T", [P, E * FJ])
        kT = sb("kT", [P, NT * P])
        qT = sb("qT", [P, NT * P])
        qbd = sb("qbd", [P, H, NT * P])
        vaug = sb("vaug", [P, NT, H, VW])
        fmin = sb("fmin", [P, S])
        fabs = sb("fabs", [P, S])
        fexp = sb("fexp", [P, S])
        fln = sb("fln", [P, S])
        cs = sb("cs", [P, S])
        am = sb("am", [P, 2, S])
        s0 = sb("s0", [P, 2, S], BF16)
        r1 = sb("r1", [P, 2, S])
        s1 = sb("s1", [P, 2, S], BF16)
        spl = sb("spl", [P, 2, S], BF16)
        m1 = sb("m1", [P, 1])
        nm = sb("nm", [P, S])
        ewn = sb("ewn", [P, 4 * P])
        tk = sb("tk", [P, 4, P])
        ek = sb("ek", [P, B, D])
        qw = sb("qw", [P, B, D])
        s1bd = sb("s1bd", [P, 2, H * VW])
        qwT = sb("qwT", [P, 2, P])
        dmat = sb("dmat", [P, 3, 512])
        ct = sb("ct", [P, 2, 512])
        osb = sb("osb", [P, 2, 4 * P])
        nrm = sb("nrm", [P, 4, 2, H])
        hh = sb("hh", [P, NT, D])
        hst = sb("hst", [P, NT, 6])
        hmv = sb("hmv", [P, NT, 2])
        hln = sb("hln", [P, NT])
        hrs = sb("hrs", [P, NT])
        tmp = sb("tmp", [P, 2, D])
        pl = sb("pl", [P, NT, 2 * D])
        st2 = sb("st2", [P, NT, 6])
        mv2 = sb("mv2", [P, NT, 2])
        ln2 = sb("ln2", [P, NT])
        rs2 = sb("rs2", [P, NT])
        xnT = sb("xnT", [P, NT * P])
        lg = sb("lg", [P, NT, E])
        mx = sb("mx", [P, NT])
        lm = sb("lm", [P, NT, E])
        ex = sb("ex", [P, NT, E])
        sm = sb("sm", [P, NT])
        rsm = sb("rsm", [P, NT])
        sc = sb("sc", [P, NT])
        scb = sb("scb", [P, 2, NT], BF16)
        scr = sb("scr", [P, 2, NT])
        enc = sb("enc", [P, NT, E])
        first = sb("first", [P, NT])
        oh = sb("oh", [P, NT, E], BF16)
        bst = sb("bst", [P, E + 1])
        t1 = sb("t1", [P, NT, E])
        t2 = sb("t2", [P, NT, E])
        slot = sb("slot", [P, NT], I32)
        grp = sb("grp", [P, NT], I32)
        off = sb("off", [P, NT], I32)
        ohg = sb("ohg", [P, NT, NT])
        ohoff = sb("ohoff", [P, NT, P], BF16)
        rv = sb("rv", [P, 2, NT, NT], BF16)
        rvs = sb("rvs", [P, NT, 3, NT], BF16)
        cv = sb("cv", [P, 2, NT])
        idx = sb("idx", [P, NT], I32)
        before = sb("before", [P, NT, E - 1])
        pos = sb("pos", [P, NT])
        gone = sb("gone", [P, Q, NT - 1])
        gq = sb("gq", [P, Q], I32)
        eq = sb("eq", [P, Q], I32)
        sq = sb("sq", [P, Q])
        past = sb("past", [P, Q, E - 1])
        es = sb("es", [P, Q])
        mine = sb("mine", [P, Q])
        gsel = sb("gsel", [P, Q, NT])
        scg = sb("scg", [P, NT])
        scq = sb("scq", [P, Q])
        msc = sb("msc", [P, Q])
        xg = sb("xg", [P, NT, 2 * D])
        xsT = sb("xsT", [P, NT * P])
        w1c = sb("w1c", [P, WBUF, F])
        hT = sb("hT", [P, 2, FJ, P])

        x_in = [sem("x_in0"), sem("x_in1")]; c_in = [sem("c_in0"), sem("c_in1")]; gw_in = sem("gw_in")
        gb_in = sem("gb_in"); gate_in = sem("gate_in"); lns_in = sem("lns_in"); sw_in = sem("sw_in")
        b1_in = sem("b1_in"); b2_in = sem("b2_in"); w1_in = [sem(f"w1_in{i}") for i in range(WBUF)]; w2_in = sem("w2_in"); 
        qbd_in = [sem(f"qbd_in{i}") for i in range(G)]
        pl_out = sem("pl_out"); xg_in = [sem(f"xg_in{i}") for i in range(NT)]; y_out = sem("y_out")
        pool_c = sem("pool_c"); sel_ok = sem("sel_ok"); b2c = sem("b2c"); gwz = sem("gwz"); dve_c = sem("dve_c")
        vaug_ok = sem("vaug_ok")
        st_ok = sem("st_ok"); mv_ok = sem("mv_ok"); lnv_ok = sem("lnv_ok"); rstd_ok = sem("rstd_ok"); xn_ok = sem("xn_ok")
        gwT_ps = sem("gwT_ps"); gwT_ok = sem("gwT_ok"); kT_ps = sem("kT_ps"); kT_ok = sem("kT_ok")
        b1T_ps = sem("b1T_ps"); b1T_ok = sem("b1T_ok")
        qT_ps = sem("qT_ps"); qT0_ok = sem("qT0_ok"); qT1_ok = sem("qT1_ok"); gate_ps = sem("gate_ps"); tg_ok = sem("tg_ok")
        fmin_ok = sem("fmin_ok"); fl_ok = sem("fl_ok"); row = sem("row"); e_ok = sem("e_ok")
        sp_ = sem("sp_"); spl_ok = sem("spl_ok"); ewn_ps = sem("ewn_ps"); tk_ok = sem("tk_ok")
        ekqw = sem("ekqw"); s1_ps = sem("s1_ps"); s1_ok = sem("s1_ok")
        qk_ps = sem("qk_ps"); arg_ps = sem("arg_ps"); d_ok = sem("d_ok");  ct_ok = sem("ct_ok")
        cv_ps = sem("cv_ps"); osb_ok = sem("osb_ok"); to_ps = sem("to_ps"); post = sem("post")
        h_ok = sem("h_ok"); hs_ok = sem("hs_ok"); hv_ok = sem("hv_ok"); hln_ok = sem("hln_ok"); hrs_ok = sem("hrs_ok")
        x2t = sem("x2t"); g1_ok = sem("g1_ok"); x2_ok = sem("x2_ok"); v2 = sem("v2"); v2_ok = sem("v2_ok")
        ln2_ok = sem("ln2_ok"); rs2_ok = sem("rs2_ok"); xn2_ok = sem("xn2_ok")
        xnT_ps = sem("xnT_ps"); xnT_ok = sem("xnT_ok"); lg_ps = sem("lg_ps"); rt = sem("rt")
        lm_ok = sem("lm_ok"); ex_ok = sem("ex_ok"); oh_ok = sem("oh_ok")
        cnt_ps = sem("cnt_ps"); rank_ps = sem("rank_ps"); rv_ok = sem("rv_ok"); inv_ps = sem("inv_ps")
        rvs_ok = sem("rvs_ok"); scg_ps = sem("scg_ps"); idx_ok = sem("idx_ok"); gq_ok = sem("gq_ok"); eq_ok = sem("eq_ok")
        xs_ps = sem("xs_ps"); xs_ok = sem("xs_ok"); h_ps = sem("h_ps")
        hT_ok = sem("hT_ok"); y_ps = sem("y_ps"); yo_ok = sem("yo_ok")

        (C_ID0, C_ID, C_PI, C_SEL0, C_SELT, C_SELA, C_SEL, C_QZ, C_MASK0, C_MASK, C_VZ, C_VONE, C_CI,
         C_BD0, C_BD1, C_BD, C_UP0, C_UP, C_ONES) = range(1, 20)

        tok_v = lambda a: a.rearrange("b (c p) d -> p (b c) d", p=P)
        block = ctx.enter_context(nc.Block())

        @block.sync
        def _(sp):
            for i in range(2):
                sp.dma_start(x_sb[:, 4 * i:4 * i + 4, :], tok_v(x)[:, 4 * i:4 * i + 4, :]).then_inc(x_in[i], 16)
            sp.dma_start(c_sb[:, 0:4, :], tok_v(ctx_in)[:, 0:4, :]).then_inc(c_in[0], 16)
            sp.wait_ge(gwz, 2)
            for base_row, w in ((0, igw), (32, fgw)):
                sp.dma_start(gw_rows[base_row:base_row + 3 * H, :],
                             w.rearrange("(a h) d -> a h d", a=1).to_broadcast([3, H, 3 * D])).then_inc(gw_in, 16)
            sp.dma_start(c_sb[:, 4:8, :], tok_v(ctx_in)[:, 4:8, :]).then_inc(c_in[1], 16)
            sp.dma_start(gbias[:, 0:1], igb.rearrange("(a h o) -> a h o", a=1, o=1).to_broadcast([P // H, H, 1])).then_inc(gb_in, 16)
            sp.dma_start(gbias[:, 1:2], fgb.rearrange("(a h o) -> a h o", a=1, o=1).to_broadcast([P // H, H, 1])).then_inc(gb_in, 16)
            sp.dma_start(b1_rows[:, :], b1.rearrange("e (j p) -> (e j) p", p=P)).then_inc(b1_in, 16)
            sp.dma_start(b2_rows[0:3 * E, :], b2.rearrange("(a e) d -> a e d", a=1).to_broadcast([3, E, D])).then_inc(b2_in, 16)
            sp.dma_start(lnsr[:, :], lns.rearrange("(a d) -> a d", a=1).to_broadcast([P, D])).then_inc(lns_in, 16)
            sp.wait_ge(pool_c, C_QZ)
            sp.wait_ge(qT0_ok, 1)
            sp.wait_ge(qT1_ok, 1)
            for h in range(H):
                sp.dma_start(qbd[DH * h:DH * (h + 1), h, :], qT[DH * h:DH * (h + 1), :]).then_inc(qbd_in[h // 4], 16)
            sp.dma_start(sw_sb[:, :], sw).then_inc(sw_in, 16)
            sp.dma_start(sbr[:, :], sb_.rearrange("(a d) -> a d", a=1).to_broadcast([P, E])).then_inc(sw_in, 16)
            sp.dma_start(w2_sb[:, :].rearrange("p (e j d) -> p e j d", e=E, j=FJ),
                         w2.rearrange("e (j p) d -> p e j d", p=P)).then_inc(w2_in, 16)
            for b in range(B):
                sp.wait_ge(xn2_ok, 2 * b + 2)
                sp.dma_start(payload.rearrange("(n p) d -> p n d", p=P)[:, 2 * b:2 * b + 2, :],
                             pl[:, 2 * b:2 * b + 2, :]).then_inc(pl_out, 16)
            sp.wait_ge(eq_ok, 1)
            for q in range(Q):
                e = sp.value_load(eq[0:1, q:q + 1], min_val=0, max_val=E - 1)
                if q >= WBUF:
                    sp.wait_ge(h_ps, q - WBUF + 1)
                sp.dma_start(w1c[:, q % WBUF, :], w1.rearrange("e d f -> d e f")[:, bass.ds(e, 1), :]).then_inc(w1_in[q % WBUF], 16)
            sp.wait_ge(y_out, 16 * NT)

        @block.gpsimd
        def _(pool):
            def c(ins):
                ins.then_inc(pool_c, 1)

            c(pool.memset(identf[:, :], 0.0))
            pool.wait_ge(pool_c, C_ID0)
            c(pool.affine_select(out=identf[:, :], in_=identf[:, :], compare_op=ALU.not_equal, fill=1.0,
                                 base=0, pattern=[[-1, P]], channel_multiplier=1))
            c(pool.iota(pi[:, :], [[0, 1]], base=0, channel_multiplier=1))
            c(pool.memset(selt[:, :, :, :], 0.0))
            pool.wait_ge(pool_c, C_SEL0)
            c(pool.affine_select(out=selt[:, :, :, :], in_=selt[:, :, :, :], compare_op=ALU.not_equal, fill=1.0,
                                 base=0, pattern=[[-32, B], [-H, 3], [-1, H]], channel_multiplier=1))
            pool.wait_ge(pool_c, C_SELT)
            c(pool.tensor_tensor(sels[:, :, :], selt[:, :, 0, :], selt[:, :, 1, :], ALU.add))
            pool.wait_ge(pool_c, C_SELA)
            c(pool.tensor_tensor(sels[:, :, :], sels[:, :, :], selt[:, :, 2, :], ALU.add))
            c(pool.memset(qbd[:, :, :], 0.0))
            c(pool.memset(mask[:, :], 0.0))
            pool.wait_ge(pool_c, C_MASK0)
            c(pool.affine_select(out=mask[:, :], in_=mask[:, :], compare_op=ALU.is_ge, fill=NEG,
                                 base=0, pattern=[[0, 4], [1, P]], channel_multiplier=-1))
            c(pool.memset(vaug[:, :, :, DH + 1:VW], 0.0))
            c(pool.memset(vaug[:, :, :, DH:DH + 1], 1.0))
            for i in range(2):
                pool.wait_ge(c_in[i], 16)
                pool.tensor_copy(vaug[:, 4 * i:4 * i + 4, :, 0:DH],
                                 c_sb[:, 4 * i:4 * i + 4, :].rearrange("p n (h d) -> p n h d", h=H)).then_inc(vaug_ok, 1)
            c(pool.iota(ci[:, :], [[1, P]], base=0, channel_multiplier=0))
            c(pool.memset(bd[:, :], 1.0))
            pool.wait_ge(pool_c, C_BD0)
            c(pool.affine_select(out=bd[:, :], in_=bd[:, :], compare_op=ALU.is_ge, fill=0.0,
                                 base=0, pattern=[[-DH, H], [0, VW]], channel_multiplier=1))
            pool.wait_ge(pool_c, C_BD1)
            c(pool.affine_select(out=bd[:, :], in_=bd[:, :], compare_op=ALU.is_ge, fill=0.0,
                                 base=DH - 1, pattern=[[DH, H], [0, VW]], channel_multiplier=-1))
            c(pool.memset(upper[:, :], 1.0))
            pool.wait_ge(pool_c, C_UP0)
            c(pool.affine_select(out=upper[:, :], in_=upper[:, :], compare_op=ALU.is_gt, fill=0.0,
                                 base=0, pattern=[[1, P]], channel_multiplier=-1))
            c(pool.memset(ones[:, :], 1.0))

            def weighted(b):
                for dst, src, w in ((ek[:, b, :], c_sb[:, 2 * b, :], 0), (qw[:, b, :], xn[:, 2 * b + 1, :], 1)):
                    pool.tensor_tensor(dst.rearrange("p (h d) -> p h d", h=H), src.rearrange("p (h d) -> p h d", h=H),
                                       tk[:, w, 32 * b:32 * b + H].unsqueeze(2).to_broadcast([P, H, DH]),
                                       ALU.mult).then_inc(ekqw, 1)

            pool.wait_ge(tk_ok, 2)
            for b in range(B):
                weighted(b)
            pool.wait_ge(pl_out, 16 * B)
            pool.wait_ge(idx_ok, 1)
            for g in range(NT):
                pool.indirect_dma_start(xg[:, g, :], None, payload, bass.IndirectOffsetOnAxis(ap=idx[:, g:g + 1], axis=0),
                                        bounds_check=B * S - 1, oob_is_err=False).then_inc(xg_in[g], 16)
            out_rows = out.rearrange("b s d -> (b s) d")
            for g in range(NT):
                pool.wait_ge(yo_ok, g + E)
                pool.indirect_dma_start(out_rows, bass.IndirectOffsetOnAxis(ap=idx[:, g:g + 1], axis=0), xg[:, g, 0:D], None,
                                        bounds_check=B * S - 1, oob_is_err=False).then_inc(y_out, 16)

        @block.scalar
        def _(act):
            act.dma_start(gate[:, 0:1], g_x.rearrange("(a o) -> a o", o=1).to_broadcast([P, 1])).then_inc(gate_in, 16)
            act.dma_start(gate[:, 1:2], g_f.rearrange("(a o) -> a o", o=1).to_broadcast([P, 1])).then_inc(gate_in, 16)
            act.wait_ge(gate_in, 32)
            act.activation(tg[:, :], gate[:, :], ACT.Tanh).then_inc(tg_ok, 1)
            act.preload_act_table_set("natural_log_exp_and_others")
            for i in range(2):
                half = slice(4 * i, 4 * i + 4)
                act.wait_ge(mv_ok, 4 * i + 4)
                act.activation(lnv[:, half], mv[:, half, 1], ACT.Ln, bias=DH * LN_EPS, scale=float(DH)).then_inc(lnv_ok, 1)
                act.wait_ge(lnv_ok, i + 1)
                act.activation(rstd[:, half], lnv[:, half], ACT.Exp, scale=-0.5).then_inc(rstd_ok, 1)
            for i in range(2):
                act.wait_ge(kT_ps, i + 1)
                act.activation(kT[:, 512 * i:512 * (i + 1)], bank[i][:, :], ACT.Copy).then_inc(kT_ok, 1)
            act.wait_ge(qT_ps, 1)
            act.activation(qT[:, 0:512], bank[2][:, :], ACT.Copy).then_inc(qT0_ok, 1)

            def spread(b0, b1_):
                act.activation(sel[:, b0:b1_, :, :].rearrange("p b h s -> p (b h) s"),
                               sels[:, b0:b1_, :].rearrange("p b h -> p (b h)").unsqueeze(2).to_broadcast([P, (b1_ - b0) * H, P]),
                               ACT.Copy).then_inc(sel_ok, 1)

            act.wait_ge(pool_c, C_SEL)
            spread(0, 2)
            act.wait_ge(gate_ps, 1)
            act.wait_ge(gb_in, 32)
            act.activation(fabs[:, :], bank[4][:, 0:S], ACT.Abs, bias=gbias[:, 1:2]).then_inc(fl_ok, 1)
            act.wait_ge(fl_ok, 1)
            act.activation(fexp[:, :], fabs[:, :], ACT.Exp, scale=-1.0).then_inc(fl_ok, 1)
            act.wait_ge(fl_ok, 2)
            act.activation(fln[:, :], fexp[:, :], ACT.Ln, bias=1.0).then_inc(fl_ok, 1)
            act.wait_ge(row, 3)
            act.activation(ewn[:, 0:P], am[:, 0, 0:P], ACT.Exp, bias=am[:, 1, P - 1:P], scale=-1.0).then_inc(e_ok, 1)
            act.wait_ge(row, 4)
            act.activation(ewn[:, P:2 * P], am[:, 1, P:S], ACT.Exp, bias=m1[:, :]).then_inc(e_ok, 1)
            act.wait_ge(row, 5)
            act.activation(ewn[:, 2 * P:4 * P], nm[:, :], ACT.Exp).then_inc(e_ok, 1)

            spread(2, B)

            def decay(u):
                act.wait_ge(arg_ps, u + 1)
                if u >= 3:
                    act.wait_ge(ct_ok, u - 2)
                act.activation(dmat[:, u % 3, :], bank[2 + u % 2][:, :], ACT.Exp).then_inc(d_ok, 1)

            def take_out(b):
                act.wait_ge(cv_ps, UB * (b + 1))
                if b >= 2:
                    act.wait_ge(to_ps, b - 1)
                act.activation(osb[:, b % 2, :], bank[4 + b % 2][:, :], ACT.Copy).then_inc(osb_ok, 1)

            def rstd_h(b):
                act.wait_ge(hv_ok, 2 * (b + 1))
                act.activation(hln[:, 2 * b:2 * b + 2], hmv[:, 2 * b:2 * b + 2, 1], ACT.Ln, bias=LN_EPS).then_inc(hln_ok, 1)
                act.wait_ge(hln_ok, b + 1)
                act.activation(hrs[:, 2 * b:2 * b + 2], hln[:, 2 * b:2 * b + 2], ACT.Exp, scale=-0.5).then_inc(hrs_ok, 1)

            def rstd_2(b):
                act.wait_ge(v2_ok, 2 * (b + 1))
                act.activation(ln2[:, 2 * b:2 * b + 2], mv2[:, 2 * b:2 * b + 2, 1], ACT.Ln, bias=LN_EPS).then_inc(ln2_ok, 1)
                act.wait_ge(ln2_ok, b + 1)
                act.activation(rs2[:, 2 * b:2 * b + 2], ln2[:, 2 * b:2 * b + 2], ACT.Exp, scale=-0.5).then_inc(rs2_ok, 1)

            def take_xnT(b):
                act.wait_ge(xnT_ps, b + 1)
                act.activation(xnT[:, S * b:S * (b + 1)], bank[6][:, 0:S], ACT.Copy).then_inc(xnT_ok, 1)

            decay(0)
            decay(1)
            for u in range(U):
                if u + 2 < U:
                    decay(u + 2)
                if u % UB == 0 and u >= UB:
                    take_out(u // UB - 1)
                if u % UB == 2 and u >= UB:
                    rstd_h(u // UB - 1)
                if u % UB == 3 and u >= UB:
                    rstd_2(u // UB - 1)
                if u % UB == 2 and u >= 2 * UB:
                    take_xnT(u // UB - 2)
            take_out(B - 1)
            take_xnT(B - 2)
            rstd_h(B - 1)
            rstd_2(B - 1)
            take_xnT(B - 1)
            act.wait_ge(lm_ok, 1)
            act.activation(ex[:, :, :], lm[:, :, :], ACT.Exp).then_inc(ex_ok, 1)
            act.preload_act_table_set("gelu_apprx_tanh_and_others")
            act.wait_ge(eq_ok, 1)
            for q in range(Q):
                e = act.value_load(eq[0:1, q:q + 1], min_val=0, max_val=E - 1)
                if q >= 2:
                    act.wait_ge(y_ps, q - 1)
                act.wait_ge(h_ps, q + 1)
                for j in range(FJ):
                    act.activation(hT[:, q % 2, j, :], bank[q % 2][:, P * j:P * (j + 1)], ACT.Gelu_apprx_tanh,
                                   bias=b1T[:, bass.ds(e * FJ + j, 1)]).then_inc(hT_ok, 1)

        @block.vector
        def _(dve):
            dve.memset(gw_rows[:, :], 0.0).then_inc(gwz, 1)
            dve.memset(b2_rows[:, :], 0.0).then_inc(gwz, 1)
            dve.memset(bst[:, 0:1], 0.0).then_inc(dve_c, 1)
            dve.memset(zero8[:, :], 0.0).then_inc(dve_c, 1)
            dve.wait_ge(pool_c, C_ID)
            dve.tensor_copy(identb[:, :], identf[:, :]).then_inc(dve_c, 1)
            dve.wait_ge(pool_c, C_PI)
            dve.tensor_copy(pf[:, :], pi[:, :]).then_inc(dve_c, 1)
            dve.tensor_scalar(jrow[:, :], pi[:, :], 24, None, ALU.bitwise_and).then_inc(dve_c, 1)
            dve.wait_ge(dve_c, 5)
            dve.tensor_scalar(kj[:, 0:1], jrow[:, :], 8.0, -1.0, ALU.is_ge, ALU.mult).then_inc(dve_c, 1)
            dve.tensor_scalar(kj[:, 1:2], jrow[:, :], 16.0, -1.0, ALU.is_ge, ALU.mult).then_inc(dve_c, 1)
            dve.tensor_scalar(kj[:, 2:3], jrow[:, :], 16.0, None, ALU.is_ge).then_inc(dve_c, 1)
            for i in range(2):
                dve.wait_ge(x_in[i], 16)
                for n in range(4 * i, 4 * i + 4):
                    dve.bn_stats(st[:, n, :], x_sb[:, n, :]).then_inc(st_ok, 1)
                for n in range(4 * i, 4 * i + 4):
                    dve.wait_ge(st_ok, n + 1)
                    dve.bn_aggr(mv[:, n, :], st[:, n, :]).then_inc(mv_ok, 1)
            for n in range(NT):
                if n % 4 == 0:
                    dve.wait_ge(rstd_ok, n // 4 + 1)
                dve.tensor_scalar(xn[:, n, :], x_sb[:, n, :], mv[:, n, 0:1], rstd[:, n:n + 1],
                                  ALU.subtract, ALU.mult).then_inc(xn_ok, 1)
            dve.wait_ge(gwT_ps, 1)
            dve.tensor_scalar(gwT[:, 0, 0:32], bank[7][:, 0:32], -4.0, None, ALU.mult).then_inc(gwT_ok, 1)
            dve.tensor_scalar(gwT[:, 0, 32:64], bank[7][:, 32:64], 4.0, None, ALU.mult).then_inc(gwT_ok, 1)
            dve.tensor_scalar(gwT[:, 1, 0:32], bank[7][:, 64:96], -1.0, None, ALU.mult).then_inc(gwT_ok, 1)
            dve.tensor_copy(gwT[:, 1, 32:64], bank[7][:, 96:128]).then_inc(gwT_ok, 1)
            dve.wait_ge(gwT_ok, 4)
            dve.tensor_tensor(gwT[:, 1, 0:32], gwT[:, 1, 0:32], bank[7][:, 128:160], ALU.subtract).then_inc(gwT_ok, 1)
            dve.tensor_tensor(gwT[:, 1, 32:64], gwT[:, 1, 32:64], bank[7][:, 160:192], ALU.add).then_inc(gwT_ok, 1)
            dve.wait_ge(qT_ps, 2)
            dve.tensor_copy(qT[:, 512:1024], bank[3][:, :]).then_inc(qT1_ok, 1)
            dve.wait_ge(b1T_ps, 1)
            dve.tensor_copy(b1T[:, :], bank[7][:, 192:192 + E * FJ]).then_inc(b1T_ok, 1)
            dve.wait_ge(gb_in, 32)
            dve.wait_ge(gate_ps, 1)
            dve.wait_ge(fl_ok, 1)
            dve.tensor_scalar(fmin[:, :], bank[4][:, 0:S], gbias[:, 1:2], 0.0, ALU.add, ALU.min).then_inc(fmin_ok, 1)
            dve.wait_ge(fmin_ok, 1)
            dve.wait_ge(fl_ok, 3)
            dve.tensor_tensor_scan(cs[:, :], fmin[:, :], fln[:, :], 0.0, ALU.add, ALU.subtract).then_inc(row, 1)
            dve.wait_ge(row, 1)
            dve.wait_ge(gate_ps, 2)
            dve.scalar_tensor_tensor(out=am[:, 0, :], in0=bank[5][:, 0:S], scalar=gbias[:, 0:1], in1=cs[:, :],
                                     op0=ALU.subtract, op1=ALU.add).then_inc(row, 1)
            dve.wait_ge(row, 2)
            dve.tensor_tensor_scan(am[:, 1, :], am[:, 0, :], am[:, 0, :], 3e38, ALU.min, ALU.min).then_inc(row, 1)
            dve.wait_ge(row, 3)
            dve.tensor_scalar(m1[:, :], am[:, 1, P - 1:P], -1.0, None, ALU.mult).then_inc(row, 1)
            dve.tensor_tensor(nm[:, :], am[:, 1, :], cs[:, :], ALU.subtract).then_inc(row, 1)
            def split(c):
                i = 3 * c
                part = slice(P * c, P * (c + 1))
                dve.tensor_copy(s0[:, :, part], am[:, :, part]).then_inc(sp_, 1)
                dve.wait_ge(sp_, i + 1)
                dve.scalar_tensor_tensor(out=r1[:, :, part], in0=s0[:, :, part], scalar=kj[:, 0:1], in1=am[:, :, part],
                                         op0=ALU.mult, op1=ALU.add).then_inc(sp_, 1)
                dve.wait_ge(sp_, i + 2)
                dve.tensor_copy(s1[:, :, part], r1[:, :, part]).then_inc(sp_, 1)
                dve.wait_ge(sp_, i + 3)
                dve.scalar_tensor_tensor(out=spl[:, 0, part], in0=s1[:, 0, part], scalar=kj[:, 2:3],
                                         in1=r1[:, 0, part], op0=ALU.mult, op1=ALU.subtract).then_inc(spl_ok, 1)
                dve.scalar_tensor_tensor(out=spl[:, 1, part], in0=s1[:, 1, part], scalar=kj[:, 1:2],
                                         in1=r1[:, 1, part], op0=ALU.mult, op1=ALU.add).then_inc(spl_ok, 1)

            dve.wait_ge(dve_c, 8)
            split(0)
            dve.wait_ge(ewn_ps, 1)
            dve.tensor_copy(tk[:, 0:2, :].rearrange("p a s -> p (a s)"), bank[6][:, 0:2 * P]).then_inc(tk_ok, 1)
            dve.tensor_copy(tk[:, 2:4, :].rearrange("p a s -> p (a s)"), bank[6][:, 2 * P:4 * P]).then_inc(tk_ok, 1)
            split(1)

            def constants():
                dve.wait_ge(tg_ok, 1)
                dve.wait_ge(lns_in, 16)
                dve.tensor_scalar(g1r[:, :], lnsr[:, :], tg[:, 0:1], None, ALU.mult).then_inc(g1_ok, 1)
                dve.wait_ge(pool_c, C_CI)
                dve.tensor_copy(cf[:, :], ci[:, :]).then_inc(dve_c, 1)
                dve.tensor_copy(cv[:, 0, :], pi[:, :].to_broadcast([P, NT])).then_inc(dve_c, 1)
                dve.wait_ge(dve_c, 10)
                dve.tensor_scalar(cv[:, 1, :], cf[:, 0:NT], float(P), None, ALU.mult).then_inc(dve_c, 1)
                dve.tensor_scalar(c128[:, :], cf[:, 0:NT], float(P), None, ALU.mult).then_inc(dve_c, 1)
                dve.tensor_scalar(dec[:, :], cf[:, 0:E], -1.0, float(E), ALU.mult, ALU.add).then_inc(dve_c, 1)
                dve.wait_ge(b2_in, 16)
                dve.tensor_copy(b2s[:, 0, :], b2_rows[:, :]).then_inc(b2c, 1)
                dve.wait_ge(b2c, 1)
                dve.scalar_tensor_tensor(out=b2t[:, :], in0=b2s[:, 0, :], scalar=kj[:, 0:1], in1=b2_rows[:, :],
                                         op0=ALU.mult, op1=ALU.add).then_inc(b2c, 1)
                dve.wait_ge(b2c, 2)
                dve.tensor_copy(b2s[:, 1, :], b2t[:, :]).then_inc(b2c, 1)
                dve.wait_ge(b2c, 3)
                dve.scalar_tensor_tensor(out=b2p[:, :], in0=b2s[:, 1, :], scalar=kj[:, 1:2], in1=b2t[:, :],
                                         op0=ALU.mult, op1=ALU.add).then_inc(b2c, 1)

            def weigh(u):
                dve.wait_ge(qk_ps, u + 1)
                dve.wait_ge(d_ok, u + 1)
                if u >= 2:
                    dve.wait_ge(cv_ps, u - 1)
                dve.tensor_tensor(ct[:, u % 2, :], bank[u % 2][:, :], dmat[:, u % 3, :], ALU.mult).then_inc(ct_ok, 1)

            def state(b):
                dve.wait_ge(s1_ps, b + 1)
                if b == 0:
                    dve.wait_ge(pool_c, C_BD)
                if b >= 2:
                    dve.wait_ge(cv_ps, UB * (b - 1))
                dve.tensor_tensor(s1bd[:, b % 2, :], bank[6][:, 0:H * VW], bd[:, :], ALU.mult).then_inc(s1_ok, 1)
                dve.tensor_copy(qwT[:, b % 2, :], bank[6][:, 256:256 + P]).then_inc(s1_ok, 1)

            def normalise(b):
                to = bank[7][:, :].rearrange("p (c h w) -> p c h w", c=2, h=H)
                dve.wait_ge(to_ps, b + 1)
                i = 4 * b
                dve.tensor_tensor(nrm[:, 0, :, :], to[:, :, :, DH], tk[:, 2:4, 32 * b:32 * b + H], ALU.max).then_inc(post, 1)
                dve.wait_ge(post, i + 1)
                dve.scalar_tensor_tensor(out=nrm[:, 1, :, :], in0=to[:, :, :, DH], scalar=-1.0, in1=nrm[:, 0, :, :],
                                         op0=ALU.mult, op1=ALU.max).then_inc(post, 1)
                dve.wait_ge(post, i + 2)
                dve.tensor_scalar(nrm[:, 2, :, :], nrm[:, 1, :, :], EPS, None, ALU.add).then_inc(post, 1)
                dve.wait_ge(post, i + 3)
                dve.reciprocal(nrm[:, 3, :, :], nrm[:, 2, :, :]).then_inc(post, 1)
                dve.wait_ge(post, i + 4)
                dve.tensor_tensor(hh[:, 2 * b:2 * b + 2, :].rearrange("p c (h d) -> p (c h) d", h=H),
                                  bank[7][:, :].rearrange("p (h w) -> p h w", w=VW)[:, :, 0:DH],
                                  nrm[:, 3, :, :].rearrange("p c h -> p (c h)").unsqueeze(2).to_broadcast([P, 2 * H, DH]),
                                  ALU.mult).then_inc(h_ok, 1)

            def spread_h(b):
                dve.wait_ge(h_ok, b + 1)
                for n in (2 * b, 2 * b + 1):
                    dve.bn_stats(hst[:, n, :], hh[:, n, :]).then_inc(hs_ok, 1)
                for n in (2 * b, 2 * b + 1):
                    dve.wait_ge(hs_ok, n + 1)
                    dve.bn_aggr(hmv[:, n, :], hst[:, n, :]).then_inc(hv_ok, 1)
                if b == 0:
                    dve.wait_ge(g1_ok, 1)
                else:
                    dve.wait_ge(x2_ok, 2 * b)
                for i in range(2):
                    n = 2 * b + i
                    dve.wait_ge(hv_ok, n + 1)
                    dve.scalar_tensor_tensor(out=tmp[:, i, :], in0=hh[:, n, :], scalar=hmv[:, n, 0:1], in1=g1r[:, :],
                                             op0=ALU.subtract, op1=ALU.mult).then_inc(x2t, 1)

            def residual(b):
                dve.wait_ge(hrs_ok, b + 1)
                for i in range(2):
                    n = 2 * b + i
                    dve.wait_ge(x2t, n + 1)
                    dve.scalar_tensor_tensor(out=pl[:, n, 0:D], in0=tmp[:, i, :], scalar=hrs[:, n:n + 1], in1=x_sb[:, n, :],
                                             op0=ALU.mult, op1=ALU.add).then_inc(x2_ok, 1)
                for n in (2 * b, 2 * b + 1):
                    dve.wait_ge(x2_ok, n + 1)
                    dve.bn_stats(st2[:, n, :], pl[:, n, 0:D]).then_inc(v2, 1)
                for n in (2 * b, 2 * b + 1):
                    dve.wait_ge(v2, n + 1)
                    dve.bn_aggr(mv2[:, n, :], st2[:, n, :]).then_inc(v2_ok, 1)

            def norm_2(b):
                dve.wait_ge(rs2_ok, b + 1)
                for n in (2 * b, 2 * b + 1):
                    dve.tensor_scalar(pl[:, n, D:2 * D], pl[:, n, 0:D], mv2[:, n, 0:1], rs2[:, n:n + 1],
                                      ALU.subtract, ALU.mult).then_inc(xn2_ok, 1)

            for u in range(U):
                weigh(u)
                if u == 2:
                    constants()
                if u % UB == 1:
                    state(u // UB)
                if u % UB == 1 and u >= UB:
                    normalise(u // UB - 1)
                if u % UB == 2 and u >= UB:
                    spread_h(u // UB - 1)
                if u % UB == 3 and u >= UB:
                    residual(u // UB - 1)
                if u % UB == 0 and u >= 2 * UB:
                    norm_2(u // UB - 2)
            norm_2(B - 2)
            normalise(B - 1)
            spread_h(B - 1)
            residual(B - 1)
            norm_2(B - 1)
            n_rt = [0]

            def link(ins):
                n_rt[0] += 1
                ins.then_inc(rt, 1)
                dve.wait_ge(rt, n_rt[0])

            rep = lambda a, k: a.unsqueeze(2).to_broadcast([P, a.shape[1], k])
            per = lambda a, k: a.unsqueeze(1).to_broadcast([P, k, a.shape[1]])
            dve.wait_ge(sw_in, 32)
            dve.wait_ge(lg_ps, B)
            link(dve.tensor_tensor(lg[:, :, :], bank[6][:, 448:512].rearrange("p (n e) -> p n e", n=NT),
                                   per(sbr[:, :], NT), ALU.add))
            link(dve.reduce_max(mx[:, :], lg[:, :, :], X))
            dve.wait_ge(dve_c, 13)
            dve.tensor_tensor(lm[:, :, :], lg[:, :, :], rep(mx[:, :], E), ALU.subtract).then_inc(lm_ok, 1)
            link(dve.tensor_tensor(enc[:, :, :], lg[:, :, :], rep(mx[:, :], E), ALU.is_equal))
            link(dve.tensor_tensor(enc[:, :, :], enc[:, :, :], per(dec[:, :], NT), ALU.mult))
            link(dve.reduce_max(first[:, :], enc[:, :, :], X))
            dve.tensor_tensor(oh[:, :, :], per(dec[:, :], NT), rep(first[:, :], E), ALU.is_equal).then_inc(oh_ok, 1)
            dve.wait_ge(ex_ok, 1)
            dve.reduce_sum(sm[:, :], ex[:, :, :], X).then_inc(rt, 1)
            n_rt[0] += 1
            dve.wait_ge(cnt_ps, 1)
            dve.wait_ge(dve_c, 2)
            link(dve.tensor_tensor_scan(bst[:, 1:E + 1], bank[0][:, 0:E], zero8[:, :], 0.0, ALU.add, ALU.add))
            dve.wait_ge(rank_ps, 1)
            link(dve.tensor_tensor(t1[:, :, :], bank[1][:, 0:NT * E].rearrange("p (n e) -> p n e", n=NT),
                                   per(bst[:, 0:E], NT), ALU.add))
            dve.wait_ge(oh_ok, 1)
            link(dve.tensor_tensor(t2[:, :, :], t1[:, :, :], oh[:, :, :], ALU.mult))
            with nc.allow_low_precision(reason="slots are whole numbers below 1024"):
                link(dve.reduce_sum(slot[:, :], t2[:, :, :], X))
            dve.tensor_scalar(off[:, :], slot[:, :], P - 1, None, ALU.bitwise_and).then_inc(rt, 1)
            n_rt[0] += 1
            link(dve.tensor_scalar(grp[:, :], slot[:, :], 7, None, ALU.logical_shift_right))
            dve.tensor_tensor(ohoff[:, :, :], rep(off[:, :], P), per(cf[:, :], NT), ALU.is_equal).then_inc(rv_ok, 1)
            link(dve.tensor_tensor(ohg[:, :, :], rep(grp[:, :], NT), per(cf[:, 0:NT], NT), ALU.is_equal))
            for c in range(2):
                dve.tensor_tensor(rv[:, c, :, :], ohg[:, :, :], rep(cv[:, c, :], NT), ALU.mult).then_inc(rv_ok, 1)
            link(dve.tensor_tensor(before[:, :, :], rep(c128[:, :], E - 1), per(bst[:, 1:E], NT), ALU.is_gt))
            dve.wait_ge(inv_ps, 1)
            dve.tensor_copy(idx[:, :], bank[2][:, 0:NT]).then_inc(idx_ok, 1)
            link(dve.reduce_sum(pos[:, :], before[:, :, :], X))
            link(dve.tensor_tensor(pos[:, :], pos[:, :], cf[:, 0:NT], ALU.add))
            link(dve.tensor_tensor(gone[:, :, :], rep(cf[:, 0:Q], NT - 1), per(pos[:, 1:NT], Q), ALU.is_ge))
            with nc.allow_low_precision(reason="counts of groups"):
                dve.reduce_sum(gq[:, :], gone[:, :, :], X).then_inc(gq_ok, 1)
            dve.wait_ge(gq_ok, 1)
            dve.tensor_tensor(eq[:, :], cf[:, 0:Q], gq[:, :], ALU.subtract).then_inc(eq_ok, 1)
            dve.wait_ge(eq_ok, 1)

            def take_rows(g):
                dve.wait_ge(xs_ps, g + 1)
                dve.tensor_copy(xsT[:, P * g:P * (g + 1)], bank[6 + g % 2][:, 0:P]).then_inc(xs_ok, 1)

            link(dve.reciprocal(rsm[:, :], sm[:, :]))
            link(dve.tensor_scalar(sc[:, :], rsm[:, :], tg[:, 1:2], None, ALU.mult))
            link(dve.tensor_copy(scb[:, 0, :], sc[:, :]))
            link(dve.tensor_tensor(scr[:, 0, :], sc[:, :], scb[:, 0, :], ALU.subtract))
            link(dve.tensor_copy(scb[:, 1, :], scr[:, 0, :]))
            link(dve.tensor_tensor(scr[:, 1, :], scr[:, 0, :], scb[:, 1, :], ALU.subtract))
            for j, part in enumerate((scb[:, 0, :], scb[:, 1, :], scr[:, 1, :])):
                dve.tensor_tensor(rvs[:, :, j, :], ohg[:, :, :], rep(part, NT), ALU.mult).then_inc(rvs_ok, 1)
            take_rows(0)
            link(dve.tensor_scalar(sq[:, :], gq[:, :], float(P), pf[:, :], ALU.mult, ALU.add))
            link(dve.tensor_tensor(past[:, :, :], rep(sq[:, :], E - 1), per(bst[:, 1:E], Q), ALU.is_ge))
            link(dve.reduce_sum(es[:, :], past[:, :, :], X))
            link(dve.tensor_tensor(mine[:, :], es[:, :], eq[:, :], ALU.is_equal))
            take_rows(1)
            link(dve.tensor_tensor(gsel[:, :, :], rep(gq[:, :], NT), per(cf[:, 0:NT], Q), ALU.is_equal))
            dve.wait_ge(scg_ps, 1)
            link(dve.reduce_sum(scg[:, :], bank[3][:, 0:3 * NT].rearrange("p (c k) -> p k c", c=3), X))
            link(dve.tensor_tensor(gsel[:, :, :], gsel[:, :, :], per(scg[:, :], Q), ALU.mult))
            link(dve.reduce_sum(scq[:, :], gsel[:, :, :], X))
            link(dve.tensor_tensor(msc[:, :], scq[:, :], mine[:, :], ALU.mult))
            for q in range(Q):
                if q + 2 < NT:
                    take_rows(q + 2)
                g = dve.value_load(gq[0:1, q:q + 1], min_val=0, max_val=NT - 1)
                dve.wait_ge(y_ps, q + 1)
                if q >= 1:
                    dve.wait_ge(yo_ok, q)
                acc = xg[:, :, :].rearrange("p g d -> p (g d)")[:, bass.ds(g * (2 * D), D)]
                dve.scalar_tensor_tensor(out=acc, in0=bank[4 + q % 2][:, 0:D], scalar=msc[:, q:q + 1], in1=acc,
                                         op0=ALU.mult, op1=ALU.add).then_inc(yo_ok, 1)

        @block.tensor
        def _(pe):
            pe.wait_ge(pool_c, C_ID)
            for n in range(4):
                if n == 0:
                    pe.wait_ge(c_in[0], 16)
                t = pe.transpose(bank[0][:, P * n:P * (n + 1)], c_sb[:, n, :], identf[:, :])
            t.then_inc(kT_ps, 1)
            pe.wait_ge(gw_in, 32)
            for i in range(3):
                t = pe.transpose(bank[7][:, 64 * i:64 * (i + 1)], gw_rows[:, D * i:D * (i + 1)], identf[0:64, 0:64])
            t.then_inc(gwT_ps, 1)
            for n in range(NT):
                if n == 4:
                    pe.wait_ge(c_in[1], 16)
                    for m in range(4):
                        t = pe.transpose(bank[1][:, P * m:P * (m + 1)], c_sb[:, 4 + m, :], identf[:, :])
                    t.then_inc(kT_ps, 1)
                pe.wait_ge(xn_ok, n + 1)
                t = pe.transpose(bank[2 + n // 4][:, P * (n % 4):P * (n % 4 + 1)], xn[:, n, :], identf[:, :])
                if n % 4 == 3:
                    t.then_inc(qT_ps, 1)
            pe.wait_ge(gwT_ok, 6)
            pe.wait_ge(kT_ok, 2)
            for part, src in ((1, kT), (0, qT)):
                if part == 0:
                    pe.wait_ge(qT0_ok, 1)
                    pe.wait_ge(qT1_ok, 1)
                for to, col in ((4, 32), (5, 0)):
                    for b in range(B):
                        t = pe.matmul(bank[to][32 * b:32 * b + 32, 0:S], gwT[:, part, col:col + 32],
                                      src[:, S * b:S * (b + 1)], start=(part == 1), stop=(part == 0), skip_group_check=True)
                    if part == 0:
                        t.then_inc(gate_ps, 1)
            pe.wait_ge(b1_in, 16)
            pe.transpose(bank[7][:, 192:192 + E * FJ], b1_rows[:, :], identf[0:E * FJ, 0:E * FJ]).then_inc(b1T_ps, 1)

            def scores(u):
                n, g = u // G, u % G
                if u >= 2:
                    pe.wait_ge(ct_ok, u - 1)
                pe.matmul(bank[u % 2][:, :], kT[:, P * n:P * (n + 1)], qbd[:, 4 * g:4 * g + 4, P * n:P * (n + 1)],
                          start=True, stop=True).then_inc(qk_ps, 1)

            def exponents(u):
                n, g = u // G, u % G
                b, c = n // 2, n % 2
                if u >= 2:
                    pe.wait_ge(d_ok, u - 1)
                to = bank[2 + u % 2]
                pe.matmul(to[:, :], identb[:, :], mask[:, :], start=True, stop=False, skip_group_check=True)
                pe.matmul(to[:, :], spl[:, 0, P * c:P * (c + 1)], sel[:, b, 4 * g:4 * g + 4, :],
                          start=False, stop=False, skip_group_check=True)
                for i in range(4):
                    t = pe.matmul(to[:, P * i:P * (i + 1)], sel[:, b, 4 * g + i, :], spl[:, 1, P * c:P * (c + 1)],
                                  start=False, stop=(i == 3), skip_group_check=True)
                t.then_inc(arg_ps, 1)

            def values(u):
                n, g = u // G, u % G
                b, c = n // 2, n % 2
                pe.wait_ge(ct_ok, u + 1)
                if g == 0 and c == 0 and b >= 2:
                    pe.wait_ge(osb_ok, b - 1)
                at = 2 * P * c + P * g
                to = bank[4 + b % 2]
                if c == 1:
                    pe.wait_ge(s1_ok, 2 * b + 2)
                    pe.matmul(to[:, at:at + P], s1bd[:, b % 2, P * g:P * (g + 1)], qwT[:, b % 2, :],
                              start=True, stop=False, skip_group_check=True)
                for i in range(4):
                    t = pe.matmul(to[32 * i:32 * i + DH + 1, at:at + P], vaug[:, n, 4 * g + i, 0:DH + 1],
                                  ct[:, u % 2, P * i:P * (i + 1)], start=(c == 0), stop=True, skip_group_check=True)
                t.then_inc(cv_ps, 1)

            def turn_back(b):
                pe.wait_ge(osb_ok, b + 1)
                if b >= 1:
                    pe.wait_ge(h_ok, b)
                else:
                    pe.wait_ge(b1T_ok, 1)
                for i in range(4):
                    t = pe.transpose(bank[7][:, P * i:P * (i + 1)], osb[:, b % 2, P * i:P * (i + 1)], identf[:, :])
                t.then_inc(to_ps, 1)

            def state(b):
                pe.wait_ge(ekqw, 2 * b + 2)
                if b >= 3:
                    pe.wait_ge(xnT_ok, b - 2)
                pe.matmul(bank[6][:, 0:H * VW], ek[:, b, :], vaug[:, 2 * b, :, :], start=True, stop=True)
                pe.transpose(bank[6][:, 256:256 + P], qw[:, b, :], identf[:, :]).then_inc(s1_ps, 1)

            def turn_normed(b):
                pe.wait_ge(xn2_ok, 2 * b + 2)
                pe.wait_ge(s1_ok, 2 * min(b + 3, B))
                for i in range(2):
                    t = pe.transpose(bank[6][:, P * i:P * (i + 1)], pl[:, 2 * b + i, D:2 * D], identf[:, :])
                t.then_inc(xnT_ps, 1)

            def logits(b):
                pe.wait_ge(xnT_ok, b + 1)
                pe.wait_ge(sw_in, 32)
                for n in (2 * b, 2 * b + 1):
                    t = pe.matmul(bank[6][:, 448 + E * n:448 + E * (n + 1)], xnT[:, P * n:P * (n + 1)], sw_sb[:, :],
                                  start=True, stop=True, skip_group_check=True)
                t.then_inc(lg_ps, 1)

            pe.wait_ge(qbd_in[0], 16 * 4)
            scores(0)
            pe.wait_ge(e_ok, 3)
            for i in range(4):
                t = pe.transpose(bank[6][:, P * i:P * (i + 1)], ewn[:, P * i:P * (i + 1)], identf[:, :])
            t.then_inc(ewn_ps, 1)
            pe.wait_ge(spl_ok, 2)
            pe.wait_ge(sel_ok, 1)
            pe.wait_ge(dve_c, 3)
            pe.wait_ge(pool_c, C_MASK)
            exponents(0)
            exponents(1)
            pe.wait_ge(qbd_in[1], 16 * 4)
            scores(1)
            pe.wait_ge(spl_ok, 4)
            pe.wait_ge(tk_ok, 2)
            pe.wait_ge(vaug_ok, 2)
            for u in range(U):
                if u + 2 < U:
                    if u + 2 == 2 * UB:
                        pe.wait_ge(sel_ok, 2)
                    exponents(u + 2)
                    scores(u + 2)
                values(u)
                if u % UB == 0:
                    state(u // UB)
                if u % UB == 0 and u >= UB:
                    turn_back(u // UB - 1)
                if u % UB == 2 and u >= 2 * UB:
                    turn_normed(u // UB - 2)
                if u % UB == 3 and u >= 2 * UB:
                    logits(u // UB - 2)
            turn_back(B - 1)
            turn_normed(B - 2)
            logits(B - 2)
            turn_normed(B - 1)
            logits(B - 1)
            pe.wait_ge(oh_ok, 1)
            pe.wait_ge(pool_c, C_ONES)
            ohf = oh[:, :, :].rearrange("p n e -> p (n e)")
            for n in range(NT):
                t = pe.matmul(bank[0][:, 0:E], ones[:, :], oh[:, n, :], start=(n == 0), stop=(n == NT - 1))
            t.then_inc(cnt_ps, 1)
            pe.matmul(bank[1][:, 0:NT * E], upper[:, :], ohf, start=True, stop=False, skip_group_check=True)
            for k in range(1, NT):
                t = pe.matmul(bank[1][:, E * k:NT * E], ones[:, :], ohf[:, 0:(NT - k) * E], start=False, stop=(k == NT - 1),
                              skip_group_check=True)
            t.then_inc(rank_ps, 1)
            pe.wait_ge(rv_ok, 3)
            for c in range(2):
                for n in range(NT):
                    t = pe.matmul(bank[2][:, 0:NT], ohoff[:, n, :], rv[:, c, n, :],
                                  start=(c == 0 and n == 0), stop=(c == 1 and n == NT - 1))
            t.then_inc(inv_ps, 1)
            pe.wait_ge(rvs_ok, 3)
            for n in range(NT):
                t = pe.matmul(bank[3][:, 0:3 * NT], ohoff[:, n, :], rvs[:, n, :, :].rearrange("p c k -> p (c k)"),
                              start=(n == 0), stop=(n == NT - 1))
            t.then_inc(scg_ps, 1)

            def rows(g):
                pe.wait_ge(xg_in[g], 16)
                if g >= 2:
                    pe.wait_ge(xs_ok, g - 1)
                pe.transpose(bank[6 + g % 2][:, 0:P], xg[:, g, D:2 * D], identf[:, :]).then_inc(xs_ps, 1)

            def up(q):
                g = pe.value_load(gq[0:1, q:q + 1], min_val=0, max_val=NT - 1)
                pe.wait_ge(xs_ok, min(q, NT - 1) + 1)
                pe.wait_ge(w1_in[q % WBUF], 16 * (q // WBUF + 1))
                if q >= 2:
                    pe.wait_ge(hT_ok, FJ * (q - 1))
                for j in range(FJ):
                    t = pe.matmul(bank[q % 2][:, P * j:P * (j + 1)], w1c[:, q % WBUF, P * j:P * (j + 1)],
                                  xsT[:, bass.ds(g * P, P)], start=True, stop=True)
                t.then_inc(h_ps, 1)

            def down(q):
                e = pe.value_load(eq[0:1, q:q + 1], min_val=0, max_val=E - 1)
                if q >= 2:
                    pe.wait_ge(yo_ok, q - 1)
                pe.matmul(bank[4 + q % 2][:, 0:D], sel[:, 0, bass.ds(e, 1), :].rearrange("p a s -> p (a s)"), b2p[:, :],
                          start=True, stop=False)
                for j in range(FJ):
                    pe.wait_ge(hT_ok, FJ * q + j + 1)
                    t = pe.matmul(bank[4 + q % 2][:, 0:D], hT[:, q % 2, j, :], w2_sb[:, bass.ds(e * F + D * j, D)],
                                  start=False, stop=(j == FJ - 1))
                t.then_inc(y_ps, 1)

            pe.wait_ge(eq_ok, 1)
            pe.wait_ge(w2_in, 16)
            pe.wait_ge(b2c, 4)
            rows(0)
            rows(1)
            for q in range(Q + 1):
                if q < Q:
                    up(q)
                if q + 2 < NT:
                    rows(q + 2)
                if q >= 1:
                    down(q - 1)


_INS = ['x', 'ctx_1024', 'g_xattn', 'g_ffn', 'L0_xattn_igate_w', 'L0_xattn_igate_b', 'L0_xattn_fgate_w',
        'L0_xattn_fgate_b', 'L0_xattn_ln_scale', 'L0_ffn_switch_w', 'L0_ffn_switch_b', 'L0_ffn_w1', 'L0_ffn_b1',
        'L0_ffn_w2', 'L0_ffn_b2']
_OUTS = [((4, 256, 128), 'float32')]


def kernel(**inputs):
    import numpy as _np
    import concourse.bacc as _bacc
    from concourse import mybir as _mybir
    from concourse.bass_utils import run_bass_kernel_spmd as _run

    nc = _bacc.Bacc("TRN2", target_bir_lowering=False, num_devices=1)
    arrays, args = {}, []
    for name in _INS:
        a = _np.ascontiguousarray(inputs[name])
        arrays[f"in_{name}_dram"] = a
        args.append(nc.dram_tensor(f"in_{name}_dram", a.shape, _mybir.dt.from_np(a.dtype), kind="ExternalInput").ap())
    for i, (shape, dtype) in enumerate(_OUTS):
        dt = _mybir.dt.from_np(_np.dtype(dtype))
        args.append(nc.dram_tensor(f"out_{i}_dram", shape, dt, kind="ExternalOutput").ap())
    gated_block(nc, *args)
    r = _run(nc, [arrays], core_ids=[0])
    got = tuple(r.results[0][f"out_{i}_dram"] for i in range(len(_OUTS)))
    return got[0]
```

```python
import math
from contextlib import ExitStack

import concourse.bass as bass
from concourse import mybir
from concourse.alu_op_type import AluOpType as ALU

ACT = mybir.ActivationFunctionType
F32 = mybir.dt.float32
BF16 = mybir.dt.bfloat16
I32 = mybir.dt.int32
X = mybir.AxisListType.X

P = 128
NEG = -1e30
LN_EPS = 1e-5
EPS = 1e-6


def gated_block(nc, x, ctx_in, g_x, g_f, igw, igb, fgw, fgb, lns, sw, sb_, w1, b1, w2, b2, out):
    B, S, D = x.shape
    H = igw.shape[0]
    DH = D // H
    E, _, F = w1.shape
    NT = B * S // P
    G = H // 4
    U = NT * G
    UB = 2 * G
    FJ = F // P
    VW = 32
    VC = DH + 1
    Q = NT + E - 1
    parts = [(2 * b, 2) for b in range(B - 1)] + [(NT - 2, 1), (NT - 1, 1)]
    POOL_Q = 2
    WARM = 7
    WBUF = 4
    assert D == P and S == 2 * P and DH == 16 and FJ == 4 and NT == 2 * B and UB == 4 and E == H

    ctx = ExitStack()
    with ctx:
        def sb(name, shape, dt=F32):
            return ctx.enter_context(nc.sbuf_tensor(name, shape, dt))

        def sem(name):
            return ctx.enter_context(nc.semaphore(name))

        bank = [ctx.enter_context(nc.psum_tensor(f"bank{i}", [P, 512], F32)) for i in range(8)]
        payload = nc.dram_tensor("payload", (B * S, 2 * D), F32, kind="Internal").ap()

        x_sb = sb("x_sb", [P, NT, D])
        c_sb = sb("c_sb", [P, NT, D])
        gw_rows = sb("gw_rows", [64, 3 * D])
        gbias = sb("gbias", [P, 2])
        gate = sb("gate", [P, 2])
        lnsr = sb("lnsr", [P, D])
        sw_sb = sb("sw_sb", [P, E])
        sbc = sb("sbc", [P, 1])
        b1_rows = sb("b1_rows", [E * FJ, P])
        b2_rows = sb("b2_rows", [P, D])
        w2_sb = sb("w2_sb", [P, E * F])
        identf = sb("identf", [P, P])
        identb = sb("identb", [P, P], BF16)
        mask = sb("mask", [P, 512], BF16)
        selt = sb("selt", [P, 3, H])
        sels = sb("sels", [P, H])
        sel = sb("sel", [P, H, P], BF16)
        sel0 = sb("sel0", [P, H, P], BF16)
        below = sb("below", [P, P], BF16)
        diag = sb("diag", [P, P], BF16)
        rm = sb("rm", [P, NT - 2, H, P], BF16)
        bd = sb("bd", [P, H, VC])
        upper = sb("upper", [P, P], BF16)
        ones = sb("ones", [P, P], BF16)
        ci = sb("ci", [P, P], I32)
        cf = sb("cf", [P, P])
        c128 = sb("c128", [P, NT])
        pi = sb("pi", [P, 1], I32)
        pf = sb("pf", [P, 1])
        dec = sb("dec", [P, E])
        jrow = sb("jrow", [P, 1], I32)
        sb_b = sb("sb_b", [P, 2], BF16)
        sb_t = sb("sb_t", [P, 2])
        sbp = sb("sbp", [P, E], BF16)
        b2s = sb("b2s", [P, 2, D], BF16)
        b2t = sb("b2t", [P, D])
        b2p = sb("b2p", [P, D], BF16)
        sg = sb("sg", [P, 2])
        turn = sb("turn", [64, 2, 64])
        kj = sb("kj", [P, 2])
        tg = sb("tg", [P, 2])
        g1r = sb("g1r", [P, D])
        st = sb("st", [P, NT, 6])
        mv = sb("mv", [P, NT, 2])
        lnv = sb("lnv", [P, NT])
        rstd = sb("rstd", [P, NT])
        xn = sb("xn", [P, NT, D])
        gwT = sb("gwT", [P, 2, 64])
        b1T = sb("b1T", [P, E * FJ])
        kT = sb("kT", [P, NT * P])
        qT = sb("qT", [P, NT * P])
        qbd = sb("qbd", [P, H, NT * P])
        vaug = sb("vaug", [P, NT, H, VW])
        fmin = sb("fmin", [P, S])
        fabs = sb("fabs", [P, S])
        fexp = sb("fexp", [P, S])
        fln = sb("fln", [P, S])
        cs = sb("cs", [P, S])
        am = sb("am", [P, 2, S])
        hat = sb("hat", [P, S], BF16)
        mh = sb("mh", [P, S])
        delta = sb("delta", [P, S])
        edel = sb("edel", [P, S])
        epst = sb("epst", [P, 2, P])
        atok = sb("atok", [P, 2, P])
        m1 = sb("m1", [P, 1])
        nm = sb("nm", [P, S])
        ewn = sb("ewn", [P, 4 * P])
        tk = sb("tk", [P, 4, P])
        ek = sb("ek", [P, B, D])
        qw = sb("qw", [P, B, D])
        s1bd = sb("s1bd", [P, 2, H, VW])
        qwT = sb("qwT", [P, 2, P])
        dmat = sb("dmat", [P, 3, 512])
        ct = sb("ct", [P, 2, 512])
        osb = sb("osb", [P, 2, 4 * P])
        nrm = sb("nrm", [P, 4, 2, H])
        hh = sb("hh", [P, NT, D])
        hst = sb("hst", [P, NT, 6])
        hmv = sb("hmv", [P, NT, 2])
        hln = sb("hln", [P, NT])
        hrs = sb("hrs", [P, NT])
        tmp = sb("tmp", [P, 2, D])
        pl = sb("pl", [P, NT, 2 * D])
        st2 = sb("st2", [P, NT, 6])
        mv2 = sb("mv2", [P, NT, 2])
        ln2 = sb("ln2", [P, NT])
        rs2 = sb("rs2", [P, NT])
        xnT = sb("xnT", [P, NT * P])
        less = sb("less", [P, NT, E], BF16)
        mx = sb("mx", [P, NT])
        lm = sb("lm", [P, NT, E])
        ex = sb("ex", [P, NT, E])
        sm = sb("sm", [P, NT])
        rsm = sb("rsm", [P, NT])
        sc = sb("sc", [P, NT])
        scb = sb("scb", [P, 2, NT], BF16)
        scr = sb("scr", [P, 2, NT])
        enc = sb("enc", [P, NT, E])
        first = sb("first", [P, NT])
        oh = sb("oh", [P, NT, E], BF16)
        bst = sb("bst", [P, E])
        t2 = sb("t2", [P, NT, E])
        slot = sb("slot", [P, NT], I32)
        grp = sb("grp", [P, NT], I32)
        off = sb("off", [P, NT], I32)
        ohg = sb("ohg", [P, NT, NT])
        ohoff = sb("ohoff", [P, NT, P], BF16)
        rv = sb("rv", [P, 2, NT, NT], BF16)
        rvs = sb("rvs", [P, NT, 3, NT], BF16)
        cv = sb("cv", [P, 2, NT])
        idx = sb("idx", [P, NT], I32)
        before = sb("before", [P, NT, E - 1])
        pos = sb("pos", [P, NT])
        gone = sb("gone", [P, Q, NT - 1])
        gq = sb("gq", [P, Q], I32)
        eq = sb("eq", [P, Q], I32)
        ep = sb("ep", [P, Q], I32)
        sq = sb("sq", [P, Q])
        past = sb("past", [P, Q, E - 1])
        es = sb("es", [P, Q])
        mine = sb("mine", [P, Q])
        gsel = sb("gsel", [P, Q, NT])
        scg = sb("scg", [P, NT])
        scq = sb("scq", [P, Q])
        msc = sb("msc", [P, Q])
        xg = sb("xg", [P, NT, 2 * D])
        xsT = sb("xsT", [P, NT * P])
        w1c = sb("w1c", [P, WBUF, F])
        hT = sb("hT", [P, 2, FJ, P])

        x_in = [sem("x_in0"), sem("x_in1")]; c_in = [sem("c_in0"), sem("c_in1")]; gw_in = sem("gw_in")
        gb_in = sem("gb_in"); gate_in = sem("gate_in"); lns_in = sem("lns_in"); sw_in = sem("sw_in")
        b1_in = sem("b1_in"); b2_in = sem("b2_in"); w2_in = sem("w2_in")
        w1_in = [sem(f"w1_in{i}") for i in range(WBUF)]
        qbd_in = [sem(f"qbd_in{i}") for i in range(G)]
        pl_out = sem("pl_out"); xg_in = [sem(f"xg_in{i}") for i in range(NT)]; y_out = sem("y_out")
        pool_c = sem("pool_c"); dve_c = sem("dve_c"); sel0_ok = sem("sel0_ok"); sel_ok = sem("sel_ok"); below_ok = sem("below_ok")
        rm_ok = sem("rm_ok"); rm_pool = sem("rm_pool"); qz_dve = sem("qz_dve"); qbd_late = sem("qbd_late"); b2c = sem("b2c")
        rm_in = [sem(f"rm_in{b}") for b in range(B)]; sbk = sem("sbk"); gwz = sem("gwz"); sg_ok = sem("sg_ok")
        vaug_ok = sem("vaug_ok")
        st_ok = sem("st_ok"); mv_ok = sem("mv_ok"); lnv_ok = sem("lnv_ok"); rstd_ok = sem("rstd_ok"); xn_ok = sem("xn_ok")
        gwT_ps = sem("gwT_ps"); gwT_ok = sem("gwT_ok"); kT_ps = sem("kT_ps"); kT_ok = sem("kT_ok")
        b1T_ps = sem("b1T_ps"); b1T_ok = sem("b1T_ok")
        qT_ps = sem("qT_ps"); qT0_ok = sem("qT0_ok"); qT1_ok = sem("qT1_ok"); gate_ps = sem("gate_ps"); tg_ok = sem("tg_ok")
        fmin_ok = sem("fmin_ok"); fl_ok = sem("fl_ok"); row = sem("row"); e_ok = sem("e_ok")
        hat_ok = sem("hat_ok"); mh_ok = sem("mh_ok"); delta_ok = sem("delta_ok"); edel_ok = sem("edel_ok"); ep_ps = sem("ep_ps"); ep_ok = sem("ep_ok"); at_ps = sem("at_ps"); at_ok = sem("at_ok"); ewn_ps = sem("ewn_ps"); tk_ok = sem("tk_ok")
        ekqw = sem("ekqw"); s1_ps = sem("s1_ps"); s1_ok = sem("s1_ok")
        qk_ps = sem("qk_ps"); arg_ps = sem("arg_ps"); d_ok = sem("d_ok");  ct_ok = sem("ct_ok")
        cv_ps = sem("cv_ps"); osb_ok = sem("osb_ok"); to_ps = sem("to_ps"); top = sem("top"); top_abs = sem("top_abs"); top_eps = sem("top_eps"); nrm_ok = sem("nrm_ok")
        h_ok = sem("h_ok"); hs_ok = sem("hs_ok"); hv_ok = sem("hv_ok"); hln_ok = sem("hln_ok"); hrs_ok = sem("hrs_ok")
        x2t = sem("x2t"); g1_ok = sem("g1_ok"); x2_ok = sem("x2_ok"); v2 = sem("v2"); v2_ok = sem("v2_ok")
        ln2_ok = sem("ln2_ok"); rs2_ok = sem("rs2_ok"); xn2_ok = sem("xn2_ok")
        xnT_ps = sem("xnT_ps"); xnT_ok = sem("xnT_ok"); lg_ps = sem("lg_ps"); rt = sem("rt")
        lm_ok = sem("lm_ok"); ex_ok = sem("ex_ok"); oh_ok = sem("oh_ok")
        cnt_ps = sem("cnt_ps"); rank_ps = sem("rank_ps"); rv_ok = sem("rv_ok"); place_ok = sem("place_ok"); ohg_ok = sem("ohg_ok"); inv_ps = sem("inv_ps")
        rvs_ok = sem("rvs_ok"); scg_ps = sem("scg_ps"); idx_ok = sem("idx_ok"); gq_ok = sem("gq_ok"); eq_ok = sem("eq_ok")
        xs_ps = sem("xs_ps"); xs_ok = sem("xs_ok"); h_ps = sem("h_ps")
        hT_ok = sem("hT_ok"); y_ps = sem("y_ps"); yo_ok = sem("yo_ok")

        (C_ID0, C_ID, C_PI, C_DIAG0, C_DIAG, C_SEL0, C_SELT, C_SELA, C_SEL, C_QZ0, C_MASK0, C_MASK, C_QZ1, C_VZ, C_VONE, 
         C_BD0, C_BD1, C_BD, C_CI, C_UP0, C_UP, C_ONES) = range(1, 23)

        v_bank = lambda n: 4 if n == NT - 1 else 4 + n // 2 % 2
        b_bank = lambda k: 7 if k < B - 1 else k - (B - 1)
        t_bank = lambda k: 6 if k < B - 1 else 2 + (k - (B - 1))
        tok_v = lambda a: a.rearrange("b (c p) d -> p (b c) d", p=P)
        block = ctx.enter_context(nc.Block())

        @block.sync
        def _(sp):
            sp.dma_start(x_sb[:, 0:4, :], tok_v(x)[:, 0:4, :]).then_inc(x_in[0], 16)
            sp.dma_start(gate[:, 1:2], g_f.rearrange("(a o) -> a o", o=1).to_broadcast([P, 1])).then_inc(gate_in, 16)
            sp.dma_start(x_sb[:, 4:8, :], tok_v(x)[:, 4:8, :]).then_inc(x_in[1], 16)
            sp.dma_start(c_sb[:, 0:4, :], tok_v(ctx_in)[:, 0:4, :]).then_inc(c_in[0], 16)
            sp.wait_ge(gwz, 2)
            for base_row, w in ((0, igw), (32, fgw)):
                sp.dma_start(gw_rows[base_row:base_row + 3 * H, :],
                             w.rearrange("(a h) d -> a h d", a=1).to_broadcast([3, H, 3 * D])).then_inc(gw_in, 16)
            sp.dma_start(c_sb[:, 4:8, :], tok_v(ctx_in)[:, 4:8, :]).then_inc(c_in[1], 16)
            sp.dma_start(gbias[:, 0:1], igb.rearrange("(a h o) -> a h o", a=1, o=1).to_broadcast([P // H, H, 1])).then_inc(gb_in, 16)
            sp.dma_start(gbias[:, 1:2], fgb.rearrange("(a h o) -> a h o", a=1, o=1).to_broadcast([P // H, H, 1])).then_inc(gb_in, 16)
            sp.dma_start(b1_rows[:, :], b1.rearrange("e (j p) -> (e j) p", p=P)).then_inc(b1_in, 16)
            sp.dma_start(b2_rows[0:3 * E, :], b2.rearrange("(a e) d -> a e d", a=1).to_broadcast([3, E, D])).then_inc(b2_in, 16)
            sp.dma_start(lnsr[:, :], lns.rearrange("(a d) -> a d", a=1).to_broadcast([P, D])).then_inc(lns_in, 16)
            sp.wait_ge(qT0_ok, 1)
            sp.wait_ge(qT1_ok, 1)
            for h in range(H - POOL_Q):
                if h % 4 == 0:
                    sp.wait_ge(pool_c, C_QZ1 if h else C_QZ0)
                sp.dma_start(qbd[DH * h:DH * (h + 1), h, :], qT[DH * h:DH * (h + 1), :]).then_inc(qbd_in[h // 4], 16)
            sp.wait_ge(hat_ok, 1)
            for b in range(1, B):
                for c in range(2):
                    sp.dma_start(rm[P - 1:P, 2 * (b - 1) + c, :, :], hat[32 * b:32 * b + H, P * c:P * (c + 1)]).then_inc(rm_in[b], 16)
            sp.dma_start(sw_sb[:, :], sw).then_inc(sw_in, 16)
            sp.dma_start(sbc[:, :], sb_.rearrange("(a h o) -> a h o", a=1, o=1).to_broadcast([P // E, E, 1])).then_inc(sw_in, 16)
            sp.dma_start(w2_sb[:, :].rearrange("p (e j d) -> p e j d", e=E, j=FJ),
                         w2.rearrange("e (j p) d -> p e j d", p=P)).then_inc(w2_in, 16)
            sp.dma_start(w1c[:, 0, :], w1[0]).then_inc(w1_in[0], 16)
            for b in range(B):
                sp.wait_ge(xn2_ok, 2 * b + 2)
                sp.dma_start(payload.rearrange("(n p) d -> p n d", p=P)[:, 2 * b:2 * b + 2, :],
                             pl[:, 2 * b:2 * b + 2, :]).then_inc(pl_out, 16)
            sp.wait_ge(eq_ok, 1)
            for q in range(1, Q):
                e = sp.value_load(eq[0:1, q:q + 1], min_val=0, max_val=E - 1)
                if q >= WBUF:
                    sp.wait_ge(h_ps, q - WBUF + 1)
                sp.dma_start(w1c[:, q % WBUF, :], w1.rearrange("e d f -> d e f")[:, bass.ds(e, 1), :]).then_inc(w1_in[q % WBUF], 16)
            sp.wait_ge(y_out, 16 * NT)

        @block.gpsimd
        def _(pool):
            def c(ins):
                ins.then_inc(pool_c, 1)

            c(pool.memset(identf[:, :], 0.0))
            pool.wait_ge(pool_c, C_ID0)
            c(pool.affine_select(out=identf[:, :], in_=identf[:, :], compare_op=ALU.not_equal, fill=1.0,
                                 base=0, pattern=[[-1, P]], channel_multiplier=1))
            c(pool.iota(pi[:, :], [[0, 1]], base=0, channel_multiplier=1))
            c(pool.memset(diag[:, :], 0.0))
            pool.wait_ge(pool_c, C_DIAG0)
            c(pool.affine_select(out=diag[:, :], in_=diag[:, :], compare_op=ALU.not_equal, fill=NEG,
                                 base=0, pattern=[[-1, P]], channel_multiplier=1))
            c(pool.memset(selt[:, :, :], 0.0))
            pool.wait_ge(pool_c, C_SEL0)
            c(pool.affine_select(out=selt[:, :, :], in_=selt[:, :, :], compare_op=ALU.not_equal, fill=1.0,
                                 base=0, pattern=[[-H, 3], [-1, H]], channel_multiplier=1))
            pool.wait_ge(pool_c, C_SELT)
            c(pool.tensor_tensor(sels[:, :], selt[:, 0, :], selt[:, 1, :], ALU.add))
            pool.wait_ge(pool_c, C_SELA)
            c(pool.tensor_tensor(sels[:, :], sels[:, :], selt[:, 2, :], ALU.add))
            pool.memset(below[:, :], 1.0).then_inc(below_ok, 1)
            pool.wait_ge(below_ok, 1)
            pool.affine_select(out=below[0:P - 1, :], in_=below[0:P - 1, :], compare_op=ALU.is_gt, fill=0.0,
                               base=0, pattern=[[1, P]], channel_multiplier=-1).then_inc(below_ok, 1)
            c(pool.memset(qbd[:, 0:4, :], 0.0))
            c(pool.memset(mask[:, :], 0.0))
            pool.wait_ge(pool_c, C_MASK0)
            c(pool.affine_select(out=mask[:, :], in_=mask[:, :], compare_op=ALU.is_ge, fill=NEG,
                                 base=0, pattern=[[0, 4], [1, P]], channel_multiplier=-1))
            c(pool.memset(qbd[:, 4:H - 1, :], 0.0))
            pool.wait_ge(qT0_ok, 1)
            pool.wait_ge(qT1_ok, 1)
            pool.wait_ge(pool_c, C_QZ1)
            for h in range(H - POOL_Q, H):
                if h == H - 1:
                    pool.wait_ge(qz_dve, 1)
                pool.dma_start(qbd[DH * h:DH * (h + 1), h, :], qT[DH * h:DH * (h + 1), :]).then_inc(qbd_late, 16)
            c(pool.memset(s1bd[:, :, :, :], 0.0))
            c(pool.memset(vaug[:, :, :, DH:DH + 1], 1.0))

            def values_of(i):
                pool.wait_ge(c_in[i], 16)
                pool.tensor_copy(vaug[:, 4 * i:4 * i + 4, :, 0:DH],
                                 c_sb[:, 4 * i:4 * i + 4, :].rearrange("p n (h d) -> p n h d", h=H)).then_inc(vaug_ok, 1)

            def weighted(b):
                for dst, src, w in ((ek[:, b, :], c_sb[:, 2 * b, :], 0), (qw[:, b, :], xn[:, 2 * b + 1, :], 1)):
                    pool.tensor_tensor(dst.rearrange("p (h d) -> p h d", h=H), src.rearrange("p (h d) -> p h d", h=H),
                                       tk[:, w, 32 * b:32 * b + H].unsqueeze(2).to_broadcast([P, H, DH]),
                                       ALU.mult).then_inc(ekqw, 1)

            values_of(0)
            c(pool.memset(bd[:, :, :], 1.0))
            pool.wait_ge(pool_c, C_BD0)
            c(pool.affine_select(out=bd[:, :, :], in_=bd[:, :, :], compare_op=ALU.is_ge, fill=0.0,
                                 base=0, pattern=[[-DH, H], [0, VC]], channel_multiplier=1))
            pool.wait_ge(pool_c, C_BD1)
            c(pool.affine_select(out=bd[:, :, :], in_=bd[:, :, :], compare_op=ALU.is_ge, fill=0.0,
                                 base=DH - 1, pattern=[[DH, H], [0, VC]], channel_multiplier=-1))
            pool.wait_ge(tk_ok, 1)
            weighted(0)
            pool.wait_ge(mh_ok, 1)
            pool.tensor_tensor(delta[:, :], mh[:, :], am[:, 1, :], ALU.subtract).then_inc(delta_ok, 1)
            c(pool.iota(ci[:, :], [[1, P]], base=0, channel_multiplier=0))
            weighted(1)
            values_of(1)
            for b in range(2, B):
                weighted(b)
            c(pool.memset(upper[:, :], 1.0))
            pool.wait_ge(pool_c, C_UP0)
            c(pool.affine_select(out=upper[:, :], in_=upper[:, :], compare_op=ALU.is_gt, fill=0.0,
                                 base=0, pattern=[[1, P]], channel_multiplier=-1))
            c(pool.memset(ones[:, :], 1.0))
            for n in (NT - 4, NT - 3):
                pool.tensor_copy(rm[0:P - 1, n, :, :], diag[0:P - 1, :].unsqueeze(1).to_broadcast([P - 1, H, P])).then_inc(rm_pool, 1)
            pool.tensor_copy(sel[:, :, :], sels[:, :].unsqueeze(2).to_broadcast([P, H, P])).then_inc(sel_ok, 1)
            pool.wait_ge(ohg_ok, 1)
            pool.wait_ge(dve_c, 8)
            for c in range(2):
                pool.tensor_tensor(rv[:, c, :, :], ohg[:, :, :], cv[:, c, :].unsqueeze(2).to_broadcast([P, NT, NT]),
                                   ALU.mult).then_inc(rv_ok, 1)
            pool.wait_ge(pl_out, 16 * B)
            pool.wait_ge(idx_ok, 1)
            for g in range(NT):
                pool.indirect_dma_start(xg[:, g, :], None, payload, bass.IndirectOffsetOnAxis(ap=idx[:, g:g + 1], axis=0),
                                        bounds_check=B * S - 1, oob_is_err=False).then_inc(xg_in[g], 16)
            out_rows = out.rearrange("b s d -> (b s) d")
            for g in range(NT):
                pool.wait_ge(yo_ok, g + E)
                pool.indirect_dma_start(out_rows, bass.IndirectOffsetOnAxis(ap=idx[:, g:g + 1], axis=0), xg[:, g, 0:D], None,
                                        bounds_check=B * S - 1, oob_is_err=False).then_inc(y_out, 16)

        @block.scalar
        def _(act):
            act.dma_start(gate[:, 0:1], g_x.rearrange("(a o) -> a o", o=1).to_broadcast([P, 1])).then_inc(gate_in, 16)
            act.wait_ge(gate_in, 32)
            act.activation(tg[:, :], gate[:, :], ACT.Tanh).then_inc(tg_ok, 1)
            act.preload_act_table_set("natural_log_exp_and_others")
            for i in range(2):
                half = slice(4 * i, 4 * i + 4)
                act.wait_ge(mv_ok, 4 * i + 4)
                act.activation(lnv[:, half], mv[:, half, 1], ACT.Ln, bias=DH * LN_EPS, scale=float(DH)).then_inc(lnv_ok, 1)
                act.wait_ge(lnv_ok, i + 1)
                act.activation(rstd[:, half], lnv[:, half], ACT.Exp, scale=-0.5).then_inc(rstd_ok, 1)

            def take_kT(i):
                act.wait_ge(kT_ps, i + 1)
                act.activation(kT[:, 512 * i:512 * (i + 1)], bank[i][:, :], ACT.Copy).then_inc(kT_ok, 1)

            take_kT(0)
            act.wait_ge(gwT_ps, 1)
            act.activation(gwT[:, :, :].rearrange("p a g -> p (a g)"), bank[7][:, 0:P], ACT.Copy).then_inc(gwT_ok, 1)
            act.wait_ge(qT_ps, 1)
            act.activation(qT[:, 0:512], bank[2][:, :], ACT.Copy).then_inc(qT0_ok, 1)
            take_kT(1)

            act.wait_ge(gate_ps, 1)
            act.wait_ge(gb_in, 32)
            act.activation(fabs[:, :], bank[4][:, 0:S], ACT.Abs, bias=gbias[:, 1:2]).then_inc(fl_ok, 1)
            act.wait_ge(fl_ok, 1)
            act.activation(fexp[:, :], fabs[:, :], ACT.Exp, scale=-1.0).then_inc(fl_ok, 1)
            act.wait_ge(fl_ok, 2)
            act.activation(fln[:, :], fexp[:, :], ACT.Ln, bias=1.0).then_inc(fl_ok, 1)
            act.wait_ge(pool_c, C_SELT)
            act.activation(sel0[:, :, :], selt[:, 0, :].unsqueeze(2).to_broadcast([P, H, P]), ACT.Copy).then_inc(sel0_ok, 1)
            act.wait_ge(at_ps, 1)
            act.activation(atok[:, :, :].rearrange("p c s -> p (c s)"), bank[7][:, 0:S], ACT.Copy, scale=-1.0).then_inc(at_ok, 1)
            act.wait_ge(mh_ok, 1)
            act.activation(ewn[:, 0:P], am[:, 0, 0:P], ACT.Exp, bias=mh[:, P - 1:P], scale=-1.0).then_inc(e_ok, 1)
            act.wait_ge(row, 4)
            act.activation(ewn[:, P:2 * P], mh[:, P:S], ACT.Exp, bias=m1[:, :]).then_inc(e_ok, 1)
            act.wait_ge(row, 5)
            act.activation(ewn[:, 2 * P:4 * P], nm[:, :], ACT.Exp).then_inc(e_ok, 1)

            act.wait_ge(at_ok, 1)

            def decay(u):
                act.wait_ge(arg_ps, u + 1)
                if u >= 3:
                    act.wait_ge(ct_ok, u - 2)
                n, g = u // G, u % G
                for i in range(4):
                    at = 32 * (n // 2) + 4 * g + i
                    act.activation(dmat[:, u % 3, P * i:P * (i + 1)], bank[2 + u % 2][:, P * i:P * (i + 1)], ACT.Exp,
                                   bias=atok[:, n % 2, at:at + 1]).then_inc(d_ok, 1)

            def take_out(k):
                n, m = parts[k]
                act.wait_ge(cv_ps, G * (n + m))
                if 2 <= k < B:
                    act.wait_ge(to_ps, k - 1)
                here = slice(2 * P * (n % 2), 2 * P * (n % 2 + m))
                act.activation(osb[:, n // 2 % 2, here], bank[v_bank(n)][:, here], ACT.Copy).then_inc(osb_ok, 1)

            def rstd_h(k):
                n, m = parts[k]
                act.wait_ge(hv_ok, n + m)
                act.activation(hln[:, n:n + m], hmv[:, n:n + m, 1], ACT.Ln, bias=LN_EPS).then_inc(hln_ok, 1)
                act.wait_ge(hln_ok, k + 1)
                act.activation(hrs[:, n:n + m], hln[:, n:n + m], ACT.Exp, scale=-0.5).then_inc(hrs_ok, 1)

            def rstd_2(k):
                n, m = parts[k]
                act.wait_ge(v2_ok, n + m)
                act.activation(ln2[:, n:n + m], mv2[:, n:n + m, 1], ACT.Ln, bias=LN_EPS).then_inc(ln2_ok, 1)
                act.wait_ge(ln2_ok, k + 1)
                act.activation(rs2[:, n:n + m], ln2[:, n:n + m], ACT.Exp, scale=-0.5).then_inc(rs2_ok, 1)

            def take_xnT(k):
                n, m = parts[k]
                act.wait_ge(xnT_ps, k + 1)
                act.activation(xnT[:, P * n:P * (n + m)], bank[t_bank(k)][:, 0:P * m], ACT.Copy).then_inc(xnT_ok, 1)

            decay(0)
            decay(1)
            for u in range(U):
                if u + 2 < U:
                    decay(u + 2)
                if u == 1:
                    act.wait_ge(delta_ok, 1)
                    act.activation(edel[:, :], delta[:, :], ACT.Exp, bias=math.log(EPS)).then_inc(edel_ok, 1)
                if u == 3:
                    act.wait_ge(ep_ps, 1)
                    act.activation(epst[:, :, :].rearrange("p c s -> p (c s)"), bank[7][:, 0:S], ACT.Copy).then_inc(ep_ok, 1)
                if u % UB == 0 and u >= UB:
                    take_out(u // UB - 1)
                if u % UB == 3 and UB <= u < U - 1:
                    rstd_h(u // UB - 1)
                if u % UB == 0 and u >= 2 * UB:
                    rstd_2(u // UB - 2)
                if u % UB == 2 and u >= 2 * UB:
                    take_xnT(u // UB - 2)
                if u == U - 3:
                    take_out(B - 1)
            take_out(B)
            rstd_h(B - 2)
            rstd_h(B - 1)
            rstd_2(B - 2)
            rstd_h(B)
            rstd_2(B - 1)
            take_xnT(B - 2)
            rstd_2(B)
            take_xnT(B - 1)
            take_xnT(B)
            act.wait_ge(lm_ok, 1)
            act.activation(ex[:, :, :], lm[:, :, :], ACT.Exp).then_inc(ex_ok, 1)
            act.preload_act_table_set("gelu_apprx_tanh_and_others")
            for q in range(Q):
                if q == 1:
                    act.wait_ge(eq_ok, 1)
                e = act.value_load(eq[0:1, q:q + 1], min_val=0, max_val=E - 1) if q else 0
                if q >= 2:
                    act.wait_ge(y_ps, q - 1)
                act.wait_ge(h_ps, q + 1)
                for j in range(FJ):
                    act.activation(hT[:, q % 2, j, :], bank[q % 3][:, P * j:P * (j + 1)], ACT.Gelu_apprx_tanh,
                                   bias=b1T[:, bass.ds(e * FJ + j, 1)]).then_inc(hT_ok, 1)

        @block.vector
        def _(dve):
            dve.memset(gw_rows[:, :], 0.0).then_inc(gwz, 1)
            dve.memset(b2_rows[:, :], 0.0).then_inc(gwz, 1)
            dve.wait_ge(pool_c, C_ID)
            dve.tensor_copy(identb[:, :], identf[:, :]).then_inc(dve_c, 1)
            dve.wait_ge(pool_c, C_PI)
            dve.tensor_copy(pf[:, :], pi[:, :]).then_inc(dve_c, 1)
            dve.tensor_scalar(jrow[:, :], pi[:, :], 24, None, ALU.bitwise_and).then_inc(dve_c, 1)
            dve.wait_ge(dve_c, 3)
            dve.tensor_scalar(kj[:, 0:1], jrow[:, :], 8.0, -1.0, ALU.is_ge, ALU.mult).then_inc(dve_c, 1)
            dve.tensor_scalar(kj[:, 1:2], jrow[:, :], 16.0, -1.0, ALU.is_ge, ALU.mult).then_inc(dve_c, 1)
            dve.tensor_scalar(sg[:, 0:1], pf[:, :], 32.0, 2.0, ALU.is_ge, ALU.mult).then_inc(sg_ok, 1)
            dve.wait_ge(sg_ok, 1)
            dve.tensor_scalar(sg[:, 1:2], sg[:, 0:1], -1.0, None, ALU.add).then_inc(sg_ok, 1)
            dve.wait_ge(sg_ok, 2)
            dve.tensor_scalar(turn[:, 0, :], identf[0:64, 0:64], sg[0:64, 1:2], 4.0, ALU.mult, ALU.mult).then_inc(sg_ok, 1)
            dve.tensor_scalar(turn[:, 1, :], identf[0:64, 0:64], sg[0:64, 1:2], None, ALU.mult).then_inc(sg_ok, 1)

            def repeat_diag(n):
                dve.tensor_copy(rm[0:P - 1, n, :, :], diag[0:P - 1, :].unsqueeze(1).to_broadcast([P - 1, H, P])).then_inc(rm_ok, 1)

            dve.wait_ge(pool_c, C_DIAG)
            repeat_diag(0)
            repeat_diag(1)
            for i in range(2):
                dve.wait_ge(x_in[i], 16)
                for n in range(4 * i, 4 * i + 4):
                    dve.bn_stats(st[:, n, :], x_sb[:, n, :]).then_inc(st_ok, 1)
                for n in range(4 * i, 4 * i + 4):
                    dve.wait_ge(st_ok, n + 1)
                    dve.bn_aggr(mv[:, n, :], st[:, n, :]).then_inc(mv_ok, 1)
            for n in range(NT):
                if n % 4 == 0:
                    dve.wait_ge(rstd_ok, n // 4 + 1)
                dve.tensor_scalar(xn[:, n, :], x_sb[:, n, :], mv[:, n, 0:1], rstd[:, n:n + 1],
                                  ALU.subtract, ALU.mult).then_inc(xn_ok, 1)
            dve.wait_ge(qT_ps, 2)
            dve.tensor_copy(qT[:, 512:1024], bank[3][:, :]).then_inc(qT1_ok, 1)
            dve.memset(qbd[:, H - 1:H, :], 0.0).then_inc(qz_dve, 1)
            dve.wait_ge(b1T_ps, 1)
            dve.tensor_copy(b1T[:, :], bank[7][:, 192:192 + E * FJ]).then_inc(b1T_ok, 1)
            dve.wait_ge(gb_in, 32)
            dve.wait_ge(gate_ps, 1)
            dve.wait_ge(fl_ok, 1)
            dve.tensor_scalar(fmin[:, :], bank[4][:, 0:S], gbias[:, 1:2], 0.0, ALU.add, ALU.min).then_inc(fmin_ok, 1)
            dve.wait_ge(fmin_ok, 1)
            dve.wait_ge(fl_ok, 3)
            dve.tensor_tensor_scan(cs[:, :], fmin[:, :], fln[:, :], 0.0, ALU.add, ALU.subtract).then_inc(row, 1)
            dve.wait_ge(row, 1)
            dve.wait_ge(gate_ps, 2)
            dve.scalar_tensor_tensor(out=am[:, 0, :], in0=bank[5][:, 0:S], scalar=gbias[:, 0:1], in1=cs[:, :],
                                     op0=ALU.subtract, op1=ALU.add).then_inc(row, 1)
            dve.wait_ge(row, 2)
            dve.tensor_tensor_scan(am[:, 1, :], am[:, 0, :], am[:, 0, :], 3e38, ALU.min, ALU.min).then_inc(row, 1)
            dve.wait_ge(row, 3)
            dve.tensor_copy(hat[:, :], am[:, 1, :]).then_inc(hat_ok, 1)
            dve.wait_ge(hat_ok, 1)
            dve.tensor_copy(mh[:, :], hat[:, :]).then_inc(mh_ok, 1)
            dve.wait_ge(mh_ok, 1)
            dve.tensor_scalar(m1[:, :], mh[:, P - 1:P], -1.0, None, ALU.mult).then_inc(row, 1)
            dve.tensor_tensor(nm[:, :], mh[:, :], cs[:, :], ALU.subtract).then_inc(row, 1)

            def constants_0():
                dve.wait_ge(tg_ok, 1)
                dve.wait_ge(lns_in, 16)
                dve.tensor_scalar(g1r[:, :], lnsr[:, :], tg[:, 0:1], None, ALU.mult).then_inc(g1_ok, 1)
                dve.wait_ge(pool_c, C_CI)
                dve.tensor_copy(cf[:, :], ci[:, :]).then_inc(dve_c, 1)
                dve.tensor_copy(cv[:, 0, :], pi[:, :].to_broadcast([P, NT])).then_inc(dve_c, 1)
                dve.wait_ge(dve_c, 7)
                dve.tensor_scalar(cv[:, 1, :], cf[:, 0:NT], float(P), None, ALU.mult).then_inc(dve_c, 1)
                dve.tensor_scalar(c128[:, :], cf[:, 0:NT], float(P), None, ALU.mult).then_inc(dve_c, 1)
                dve.tensor_scalar(dec[:, :], cf[:, 0:E], -1.0, float(E), ALU.mult, ALU.add).then_inc(dve_c, 1)

            def constants_1():
                dve.wait_ge(sw_in, 32)
                dve.wait_ge(dve_c, 5)
                dve.wait_ge(pool_c, C_SEL)
                dve.tensor_copy(sb_b[:, 0:1], sbc[:, :]).then_inc(sbk, 1)
                dve.wait_ge(sbk, 1)
                dve.scalar_tensor_tensor(out=sb_t[:, 0:1], in0=sb_b[:, 0:1], scalar=kj[:, 0:1], in1=sbc[:, :],
                                         op0=ALU.mult, op1=ALU.add).then_inc(sbk, 1)
                dve.wait_ge(sbk, 2)
                dve.tensor_copy(sb_b[:, 1:2], sb_t[:, 0:1]).then_inc(sbk, 1)
                dve.wait_ge(sbk, 3)
                dve.scalar_tensor_tensor(out=sb_t[:, 1:2], in0=sb_b[:, 1:2], scalar=kj[:, 1:2], in1=sb_t[:, 0:1],
                                         op0=ALU.mult, op1=ALU.add).then_inc(sbk, 1)
                dve.wait_ge(sbk, 4)
                dve.tensor_scalar(sbp[:, :], sels[:, :], sb_t[:, 1:2], None, ALU.mult).then_inc(sbk, 1)

            def constants_2():
                dve.wait_ge(b2_in, 16)
                dve.tensor_copy(b2s[:, 0, :], b2_rows[:, :]).then_inc(b2c, 1)
                dve.wait_ge(b2c, 1)
                dve.scalar_tensor_tensor(out=b2t[:, :], in0=b2s[:, 0, :], scalar=kj[:, 0:1], in1=b2_rows[:, :],
                                         op0=ALU.mult, op1=ALU.add).then_inc(b2c, 1)
                dve.wait_ge(b2c, 2)
                dve.tensor_copy(b2s[:, 1, :], b2t[:, :]).then_inc(b2c, 1)
                dve.wait_ge(b2c, 3)
                dve.scalar_tensor_tensor(out=b2p[:, :], in0=b2s[:, 1, :], scalar=kj[:, 1:2], in1=b2t[:, :],
                                         op0=ALU.mult, op1=ALU.add).then_inc(b2c, 1)

            def weigh(u):
                dve.wait_ge(qk_ps, u + 1)
                dve.wait_ge(d_ok, 4 * (u + 1))
                if u >= 2:
                    dve.wait_ge(cv_ps, u - 1)
                dve.tensor_tensor(ct[:, u % 2, :], bank[u % 2][:, :], dmat[:, u % 3, :], ALU.mult).then_inc(ct_ok, 1)

            def state(b):
                dve.wait_ge(s1_ps, b + 1)
                if b == 0:
                    dve.wait_ge(pool_c, C_BD)
                if b >= 2:
                    dve.wait_ge(cv_ps, UB * (b - 1))
                dve.tensor_tensor(s1bd[:, b % 2, :, 0:VC], bank[6][:, 0:H * VC].rearrange("p (h w) -> p h w", h=H), bd[:, :, :], ALU.mult).then_inc(s1_ok, 1)
                dve.tensor_copy(qwT[:, b % 2, :], bank[6][:, 256:256 + P]).then_inc(s1_ok, 1)

            def greatest(k, step):
                n, m = parts[k]
                c = n % 2
                here = slice(c, c + m)
                total = bank[b_bank(k)][:, 2 * P * c:2 * P * (c + m)].rearrange("p (c h w) -> p c h w", c=m, h=H)[:, :, :, DH]
                if step == 0:
                    dve.wait_ge(to_ps, k + 1)
                    dve.tensor_tensor(nrm[:, 0, here, :], total, tk[:, 2 + c:2 + c + m, 16 * n - 16 * c:16 * n - 16 * c + H],
                                      ALU.max).then_inc(top, 1)
                elif step == 1:
                    dve.wait_ge(top, k + 1)
                    dve.scalar_tensor_tensor(out=nrm[:, 1, here, :], in0=total, scalar=-1.0, in1=nrm[:, 0, here, :],
                                             op0=ALU.mult, op1=ALU.max).then_inc(top_abs, 1)
                elif step == 2:
                    dve.wait_ge(top_abs, k + 1)
                    dve.wait_ge(ep_ok, 1)
                    dve.tensor_tensor(nrm[:, 2, here, :], nrm[:, 1, here, :], epst[:, here, 16 * n - 16 * c:16 * n - 16 * c + H],
                                      ALU.add).then_inc(top_eps, 1)
                else:
                    dve.wait_ge(top_eps, k + 1)
                    dve.reciprocal(nrm[:, 3, here, :], nrm[:, 2, here, :]).then_inc(nrm_ok, 1)

            def divide(k):
                n, m = parts[k]
                c = n % 2
                dve.wait_ge(nrm_ok, k + 1)
                dve.tensor_tensor(hh[:, n:n + m, :].rearrange("p c (h d) -> p (c h) d", h=H),
                                  bank[b_bank(k)][:, 2 * P * c:2 * P * (c + m)].rearrange("p (h w) -> p h w", w=VW)[:, :, 0:DH],
                                  nrm[:, 3, c:c + m, :].rearrange("p c h -> p (c h)").unsqueeze(2).to_broadcast([P, m * H, DH]),
                                  ALU.mult).then_inc(h_ok, 1)

            def stats_h(k):
                n0, m = parts[k]
                dve.wait_ge(h_ok, k + 1)
                for n in range(n0, n0 + m):
                    dve.bn_stats(hst[:, n, :], hh[:, n, :]).then_inc(hs_ok, 1)

            def aggr_h(k):
                n0, m = parts[k]
                for n in range(n0, n0 + m):
                    dve.wait_ge(hs_ok, n + 1)
                    dve.bn_aggr(hmv[:, n, :], hst[:, n, :]).then_inc(hv_ok, 1)

            def centre_h(k):
                n0, m = parts[k]
                if k == 0:
                    dve.wait_ge(g1_ok, 1)
                for n in range(n0, n0 + m):
                    if n >= 2:
                        dve.wait_ge(x2_ok, n - 1)
                    dve.wait_ge(hv_ok, n + 1)
                    dve.scalar_tensor_tensor(out=tmp[:, n % 2, :], in0=hh[:, n, :], scalar=hmv[:, n, 0:1], in1=g1r[:, :],
                                             op0=ALU.subtract, op1=ALU.mult).then_inc(x2t, 1)

            def add_x(k):
                n0, m = parts[k]
                dve.wait_ge(hrs_ok, k + 1)
                for n in range(n0, n0 + m):
                    dve.wait_ge(x2t, n + 1)
                    dve.scalar_tensor_tensor(out=pl[:, n, 0:D], in0=tmp[:, n % 2, :], scalar=hrs[:, n:n + 1], in1=x_sb[:, n, :],
                                             op0=ALU.mult, op1=ALU.add).then_inc(x2_ok, 1)

            def stats_2(k):
                n0, m = parts[k]
                for n in range(n0, n0 + m):
                    dve.wait_ge(x2_ok, n + 1)
                    dve.bn_stats(st2[:, n, :], pl[:, n, 0:D]).then_inc(v2, 1)

            def aggr_2(k):
                n0, m = parts[k]
                for n in range(n0, n0 + m):
                    dve.wait_ge(v2, n + 1)
                    dve.bn_aggr(mv2[:, n, :], st2[:, n, :]).then_inc(v2_ok, 1)

            def norm_2(k):
                n0, m = parts[k]
                dve.wait_ge(rs2_ok, k + 1)
                for n in range(n0, n0 + m):
                    dve.tensor_scalar(pl[:, n, D:2 * D], pl[:, n, 0:D], mv2[:, n, 0:1], rs2[:, n:n + 1],
                                      ALU.subtract, ALU.mult).then_inc(xn2_ok, 1)

            def spread_h(k):
                stats_h(k)
                aggr_h(k)
                centre_h(k)

            def residual(k):
                add_x(k)
                stats_2(k)
                aggr_2(k)

            for u in range(U):
                weigh(u)
                if u == 0:
                    dve.wait_ge(ewn_ps, 1)
                    dve.tensor_copy(tk[:, 0:2, :].rearrange("p a s -> p (a s)"), bank[6][:, 0:2 * P]).then_inc(tk_ok, 1)
                    dve.tensor_copy(tk[:, 2:4, :].rearrange("p a s -> p (a s)"), bank[6][:, 2 * P:4 * P]).then_inc(tk_ok, 1)
                if u == 2:
                    constants_0()
                if u == 4 or u == 5:
                    repeat_diag(u - 2)
                if u == 3:
                    constants_1()
                if u == 3:
                    constants_2()
                if u % UB == 1:
                    state(u // UB)
                if u % UB == 2 and UB <= u < U - UB:
                    for step in range(4):
                        greatest(u // UB - 1, step)
                if u % UB == 3 and UB <= u < U - UB:
                    divide(u // UB - 1)
                    spread_h(u // UB - 1)
                if u % UB == 0 and u >= 2 * UB:
                    residual(u // UB - 2)
                if u % UB == 1 and u >= 2 * UB:
                    norm_2(u // UB - 2)
            y, z, l = B - 2, B - 1, B
            for step in range(4):
                greatest(y, step)
            divide(y)
            greatest(z, 0)
            stats_h(y)
            greatest(z, 1)
            aggr_h(y)
            greatest(z, 2)
            centre_h(y)
            greatest(z, 3)
            greatest(l, 0)
            divide(z)
            greatest(l, 1)
            add_x(y)
            stats_h(z)
            greatest(l, 2)
            stats_2(y)
            aggr_h(z)
            greatest(l, 3)
            aggr_2(y)
            centre_h(z)
            divide(l)
            add_x(z)
            stats_h(l)
            norm_2(y)
            stats_2(z)
            aggr_h(l)
            aggr_2(z)
            centre_h(l)
            add_x(l)
            stats_2(l)
            aggr_2(l)
            norm_2(z)
            norm_2(l)
            n_rt = [0]

            def link(ins):
                n_rt[0] += 1
                ins.then_inc(rt, 1)
                dve.wait_ge(rt, n_rt[0])

            rep = lambda a, k: a.unsqueeze(2).to_broadcast([P, a.shape[1], k])
            per = lambda a, k: a.unsqueeze(1).to_broadcast([P, k, a.shape[1]])
            dve.wait_ge(lg_ps, len(parts))
            lg = bank[6][:, 448:512].rearrange("p (n e) -> p n e", n=NT)
            link(dve.reduce_max(mx[:, :], lg, X))
            dve.wait_ge(dve_c, 10)
            link(dve.tensor_tensor(enc[:, :, :], lg, rep(mx[:, :], E), ALU.is_equal))
            link(dve.tensor_tensor(enc[:, :, :], enc[:, :, :], per(dec[:, :], NT), ALU.mult))
            link(dve.reduce_max(first[:, :], enc[:, :, :], X))
            dve.tensor_tensor(oh[:, :, :], per(dec[:, :], NT), rep(first[:, :], E), ALU.is_equal).then_inc(oh_ok, 1)
            dve.tensor_tensor(less[:, :, :], per(dec[:, :], NT), rep(first[:, :], E), ALU.is_lt).then_inc(oh_ok, 1)
            dve.tensor_tensor(lm[:, :, :], lg, rep(mx[:, :], E), ALU.subtract).then_inc(lm_ok, 1)
            dve.wait_ge(oh_ok, 1)
            dve.wait_ge(rank_ps, 1)
            link(dve.tensor_tensor(t2[:, :, :], bank[1][:, 0:NT * E].rearrange("p (n e) -> p n e", n=NT), oh[:, :, :], ALU.mult))
            with nc.allow_low_precision(reason="slots are whole numbers below 1024"):
                link(dve.reduce_sum(slot[:, :], t2[:, :, :], X))
            dve.tensor_scalar(grp[:, :], slot[:, :], 7, None, ALU.logical_shift_right).then_inc(place_ok, 1)
            dve.tensor_scalar(off[:, :], slot[:, :], P - 1, None, ALU.bitwise_and).then_inc(place_ok, 1)
            dve.wait_ge(place_ok, 1)
            dve.tensor_tensor(ohg[:, :, :], rep(grp[:, :], NT), per(cf[:, 0:NT], NT), ALU.is_equal).then_inc(ohg_ok, 1)
            dve.wait_ge(place_ok, 2)
            dve.tensor_tensor(ohoff[:, :, :], rep(off[:, :], P), per(cf[:, :], NT), ALU.is_equal).then_inc(rv_ok, 1)
            dve.wait_ge(cnt_ps, 1)
            link(dve.tensor_copy(bst[:, :], bank[0][:, 0:E]))
            link(dve.tensor_tensor(before[:, :, :], rep(c128[:, :], E - 1), per(bst[:, 1:E], NT), ALU.is_gt))
            link(dve.reduce_sum(pos[:, :], before[:, :, :], X))
            dve.wait_ge(inv_ps, 1)
            dve.tensor_copy(idx[:, :], bank[2][:, 0:NT]).then_inc(idx_ok, 1)
            link(dve.tensor_tensor(pos[:, :], pos[:, :], cf[:, 0:NT], ALU.add))
            link(dve.tensor_tensor(gone[:, :, :], rep(cf[:, 0:Q], NT - 1), per(pos[:, 1:NT], Q), ALU.is_ge))
            with nc.allow_low_precision(reason="counts of groups"):
                dve.reduce_sum(gq[:, :], gone[:, :, :], X).then_inc(gq_ok, 1)
            dve.wait_ge(gq_ok, 1)
            dve.tensor_tensor(eq[:, :], cf[:, 0:Q], gq[:, :], ALU.subtract).then_inc(eq_ok, 1)
            dve.wait_ge(eq_ok, 1)
            dve.tensor_scalar(ep[:, :], eq[:, :], float(P), None, ALU.mult).then_inc(eq_ok, 1)

            def take_rows(g):
                dve.wait_ge(xs_ps, g + 1)
                dve.tensor_copy(xsT[:, P * g:P * (g + 1)], bank[6 + g % 2][:, 0:P]).then_inc(xs_ok, 1)

            dve.wait_ge(ex_ok, 1)
            link(dve.reduce_sum(sm[:, :], ex[:, :, :], X))
            link(dve.reciprocal(rsm[:, :], sm[:, :]))
            link(dve.tensor_scalar(sc[:, :], rsm[:, :], tg[:, 1:2], None, ALU.mult))
            link(dve.tensor_copy(scb[:, 0, :], sc[:, :]))
            link(dve.tensor_tensor(scr[:, 0, :], sc[:, :], scb[:, 0, :], ALU.subtract))
            link(dve.tensor_copy(scb[:, 1, :], scr[:, 0, :]))
            link(dve.tensor_tensor(scr[:, 1, :], scr[:, 0, :], scb[:, 1, :], ALU.subtract))
            dve.wait_ge(ohg_ok, 1)
            for j, part in enumerate((scb[:, 0, :], scb[:, 1, :], scr[:, 1, :])):
                dve.tensor_tensor(rvs[:, :, j, :], ohg[:, :, :], rep(part, NT), ALU.mult).then_inc(rvs_ok, 1)
            take_rows(0)
            link(dve.tensor_scalar(sq[:, :], gq[:, :], float(P), pf[:, :], ALU.mult, ALU.add))
            link(dve.tensor_tensor(past[:, :, :], rep(sq[:, :], E - 1), per(bst[:, 1:E], Q), ALU.is_ge))
            link(dve.reduce_sum(es[:, :], past[:, :, :], X))
            link(dve.tensor_tensor(mine[:, :], es[:, :], eq[:, :], ALU.is_equal))
            take_rows(1)
            link(dve.tensor_tensor(gsel[:, :, :], rep(gq[:, :], NT), per(cf[:, 0:NT], Q), ALU.is_equal))
            dve.wait_ge(scg_ps, 1)
            link(dve.reduce_sum(scg[:, :], bank[3][:, 0:3 * NT].rearrange("p (c k) -> p k c", c=3), X))
            link(dve.tensor_tensor(gsel[:, :, :], gsel[:, :, :], per(scg[:, :], Q), ALU.mult))
            link(dve.reduce_sum(scq[:, :], gsel[:, :, :], X))
            link(dve.tensor_tensor(msc[:, :], scq[:, :], mine[:, :], ALU.mult))
            for q in range(Q):
                if q + 2 < NT:
                    take_rows(q + 2)
                g = dve.value_load(gq[0:1, q:q + 1], min_val=0, max_val=NT - 1)
                dve.wait_ge(y_ps, q + 1)
                if q >= 1:
                    dve.wait_ge(yo_ok, q)
                acc = xg[:, :, :].rearrange("p g d -> p (g d)")[:, bass.ds(g * (2 * D), D)]
                dve.scalar_tensor_tensor(out=acc, in0=bank[4 + q % 2][:, 0:D], scalar=msc[:, q:q + 1], in1=acc,
                                         op0=ALU.mult, op1=ALU.add).then_inc(yo_ok, 1)

        @block.tensor
        def _(pe):
            pe.wait_ge(pool_c, C_ID)

            def keep_warm(k, to):
                for _ in range(k):
                    pe.matmul(bank[to][:, 0:P], identf[:, :], identf[:, :], start=True, stop=True)

            keep_warm(9, 6)
            pe.wait_ge(c_in[0], 16)
            for n in range(4):
                t = pe.transpose(bank[0][:, P * n:P * (n + 1)], c_sb[:, n, :], identf[:, :])
            t.then_inc(kT_ps, 1)
            pe.wait_ge(gw_in, 32)
            pe.wait_ge(sg_ok, 4)
            pe.matmul(bank[7][:, 0:64], gw_rows[:, 0:D], turn[:, 0, :], start=True, stop=True)
            pe.matmul(bank[7][:, 64:P], gw_rows[:, D:2 * D], turn[:, 1, :], start=True, stop=False)
            pe.matmul(bank[7][:, 64:P], gw_rows[:, 2 * D:3 * D], turn[:, 1, :], start=False, stop=True).then_inc(gwT_ps, 1)
            for n in range(NT):
                pe.wait_ge(xn_ok, n + 1)
                t = pe.transpose(bank[2 + n // 4][:, P * (n % 4):P * (n % 4 + 1)], xn[:, n, :], identf[:, :])
                if n % 4 == 3:
                    t.then_inc(qT_ps, 1)
            pe.wait_ge(c_in[1], 16)
            for n in range(4):
                t = pe.transpose(bank[1][:, P * n:P * (n + 1)], c_sb[:, 4 + n, :], identf[:, :])
            t.then_inc(kT_ps, 1)
            pe.wait_ge(gwT_ok, 1)
            pe.wait_ge(b1_in, 16)
            pe.transpose(bank[7][:, 192:192 + E * FJ], b1_rows[:, :], identf[0:E * FJ, 0:E * FJ]).then_inc(b1T_ps, 1)
            for to, col in ((4, 32), (5, 0)):
                for half, q_ok in ((0, qT0_ok), (1, qT1_ok)):
                    pe.wait_ge(q_ok, 1)
                    for part, src in ((0, qT), (1, kT)):
                        if part == 1:
                            pe.wait_ge(kT_ok, half + 1)
                        for b in (2 * half, 2 * half + 1):
                            t = pe.matmul(bank[to][32 * b:32 * b + 32, 0:S], gwT[:, part, col:col + 32],
                                          src[:, S * b:S * (b + 1)], start=(part == 0), stop=(part == 1), skip_group_check=True)
                t.then_inc(gate_ps, 1)
            keep_warm(7, 6)

            def scores(u):
                n, g = u // G, u % G
                if u >= 2:
                    pe.wait_ge(ct_ok, u - 1)
                pe.matmul(bank[u % 2][:, :], kT[:, P * n:P * (n + 1)], qbd[:, 4 * g:4 * g + 4, P * n:P * (n + 1)],
                          start=True, stop=True).then_inc(qk_ps, 1)

            def exponents(u):
                n, g = u // G, u % G
                b, c = n // 2, n % 2
                if u >= 2:
                    pe.wait_ge(d_ok, 4 * (u - 1))
                to = bank[2 + u % 2]
                if b == 0:
                    pe.matmul(to[:, :], identb[:, :], mask[:, :], start=True, stop=False, skip_group_check=True)
                    for i in range(4):
                        t = pe.matmul(to[:, P * i:P * (i + 1)], sel0[:, 4 * g + i, :], hat[:, P * c:P * (c + 1)],
                                      start=False, stop=(i == 3), skip_group_check=True)
                else:
                    t = pe.matmul(to[:, :], below[:, :], rm[:, n - 2, 4 * g:4 * g + 4, :], start=True, stop=True, skip_group_check=True)
                t.then_inc(arg_ps, 1)

            def values(u):
                n, g = u // G, u % G
                b, c = n // 2, n % 2
                pe.wait_ge(ct_ok, u + 1)
                if n == NT // 2:
                    pe.wait_ge(vaug_ok, 2)
                if g == 0 and c == 0 and b >= 2:
                    pe.wait_ge(osb_ok, b - 1)
                if g == 0 and n == NT - 1:
                    pe.wait_ge(osb_ok, B - 1)
                at = 2 * P * c + P * g
                to = bank[v_bank(n)]
                if c == 1:
                    pe.wait_ge(s1_ok, 2 * b + 2)
                    pe.matmul(to[:, at:at + P], s1bd[:, b % 2, 4 * g:4 * g + 4, :], qwT[:, b % 2, :],
                              start=True, stop=False, skip_group_check=True)
                for i in range(4):
                    t = pe.matmul(to[32 * i:32 * i + VC, at:at + P], vaug[:, n, 4 * g + i, 0:VC],
                                  ct[:, u % 2, P * i:P * (i + 1)], start=(c == 0), stop=True, skip_group_check=True)
                t.then_inc(cv_ps, 1)

            def turn_back(k):
                n, m = parts[k]
                pe.wait_ge(osb_ok, k + 1)
                if k == 0:
                    pe.wait_ge(ep_ok, 1)
                elif k < B - 1:
                    pe.wait_ge(h_ok, k)
                else:
                    pe.wait_ge(ct_ok, U)
                for i in range(2 * (n % 2), 2 * (n % 2 + m)):
                    t = pe.transpose(bank[b_bank(k)][:, P * i:P * (i + 1)], osb[:, n // 2 % 2, P * i:P * (i + 1)], identf[:, :])
                t.then_inc(to_ps, 1)

            def state(b):
                pe.wait_ge(ekqw, 2 * b + 2)
                if b == 0:
                    pe.wait_ge(tk_ok, 2)
                if b >= 3:
                    pe.wait_ge(xnT_ok, b - 2)
                pe.matmul(bank[6][:, 0:H * VC], ek[:, b, :], vaug[:, 2 * b, :, 0:VC], start=True, stop=True)
                pe.transpose(bank[6][:, 256:256 + P], qw[:, b, :], identf[:, :]).then_inc(s1_ps, 1)

            def turn_normed(k):
                n, m = parts[k]
                pe.wait_ge(xn2_ok, n + m)
                if k < B - 1:
                    pe.wait_ge(s1_ok, 2 * min(k + 3, B))
                else:
                    pe.wait_ge(d_ok, 4 * U)
                for i in range(m):
                    t = pe.transpose(bank[t_bank(k)][:, P * i:P * (i + 1)], pl[:, n + i, D:2 * D], identf[:, :])
                t.then_inc(xnT_ps, 1)

            def logits_bias(n, m):
                pe.matmul(bank[6][:, 448 + E * n:448 + E * (n + m)], ones[:, :],
                          sbp[:, :].unsqueeze(1).to_broadcast([P, m, E]), start=True, stop=False, skip_group_check=True)

            def logits(k):
                n0, m = parts[k]
                pe.wait_ge(xnT_ok, k + 1)
                if k < B - 1:
                    logits_bias(n0, m)
                for n in range(n0, n0 + m):
                    at = 448 + E * n
                    t = pe.matmul(bank[6][:, at:at + E], xnT[:, P * n:P * (n + 1)], sw_sb[:, :],
                                  start=False, stop=True, skip_group_check=True)
                t.then_inc(lg_ps, 1)

            pe.wait_ge(row, 2)
            pe.wait_ge(b1T_ok, 1)
            for c in range(2):
                t = pe.transpose(bank[7][:, P * c:P * (c + 1)], am[:, 0, P * c:P * (c + 1)], identf[:, :])
            t.then_inc(at_ps, 1)
            keep_warm(2, 6)
            pe.wait_ge(hat_ok, 1)
            pe.wait_ge(sel0_ok, 1)
            pe.wait_ge(dve_c, 1)
            pe.wait_ge(pool_c, C_MASK)
            exponents(0)
            pe.wait_ge(qbd_in[0], 16 * 4)
            scores(0)
            exponents(1)
            pe.wait_ge(e_ok, 3)
            for i in range(4):
                t = pe.transpose(bank[6][:, P * i:P * (i + 1)], ewn[:, P * i:P * (i + 1)], identf[:, :])
            t.then_inc(ewn_ps, 1)
            pe.wait_ge(qbd_in[1], 16 * (4 - POOL_Q))
            pe.wait_ge(qbd_late, 16 * POOL_Q)
            scores(1)
            pe.wait_ge(vaug_ok, 1)
            for u in range(U):
                if u + 2 < U:
                    if (u + 2) % UB == 0:
                        b = (u + 2) // UB
                        pe.wait_ge(rm_in[b], 32)
                        if b < B - 1:
                            pe.wait_ge(rm_ok, 2 * b)
                        else:
                            pe.wait_ge(rm_pool, 2)
                        pe.wait_ge(below_ok, 2)
                    exponents(u + 2)
                    scores(u + 2)
                values(u)
                if u % UB == 0:
                    state(u // UB)
                if u % UB == 1 and u >= UB:
                    turn_back(u // UB - 1)
                if u == 2 * UB:
                    pe.wait_ge(sw_in, 32)
                    pe.wait_ge(sbk, 5)
                    pe.wait_ge(pool_c, C_ONES)
                if u == 2:
                    pe.wait_ge(edel_ok, 1)
                    pe.wait_ge(at_ok, 1)
                    for c in range(2):
                        t = pe.transpose(bank[7][:, P * c:P * (c + 1)], edel[:, P * c:P * (c + 1)], identf[:, :])
                    t.then_inc(ep_ps, 1)
                if u % UB == 2 and u >= 2 * UB:
                    turn_normed(u // UB - 2)
                if u == U - 1:
                    turn_back(B - 1)
                if u % UB == 3 and u >= 2 * UB:
                    logits(u // UB - 2)
            turn_back(B)
            turn_normed(B - 2)
            logits(B - 2)
            logits_bias(NT - 2, 2)
            turn_normed(B - 1)
            turn_normed(B)
            logits(B - 1)
            logits(B)
            ohf = oh[:, :, :].rearrange("p n e -> p (n e)")
            pe.wait_ge(oh_ok, 1)
            pe.matmul(bank[1][:, 0:NT * E], upper[:, :], ohf, start=True, stop=False, skip_group_check=True)
            for k in range(1, NT):
                pe.matmul(bank[1][:, E * k:NT * E], ones[:, :], ohf[:, 0:(NT - k) * E], start=False, stop=False,
                          skip_group_check=True)
            pe.wait_ge(oh_ok, 2)
            for n in range(NT):
                t = pe.matmul(bank[1][:, 0:NT * E].rearrange("p (n e) -> p n e", n=NT), ones[:, :],
                              less[:, n, :].unsqueeze(1).to_broadcast([P, NT, E]), start=False, stop=(n == NT - 1),
                              skip_group_check=True)
            t.then_inc(rank_ps, 1)
            for n in range(NT):
                t = pe.matmul(bank[0][:, 0:E], ones[:, :], less[:, n, :], start=(n == 0), stop=(n == NT - 1))
            t.then_inc(cnt_ps, 1)
            keep_warm(4, 5)
            pe.wait_ge(rv_ok, 3)
            for c in range(2):
                for n in range(NT):
                    t = pe.matmul(bank[2][:, 0:NT], ohoff[:, n, :], rv[:, c, n, :],
                                  start=(c == 0 and n == 0), stop=(c == 1 and n == NT - 1))
            t.then_inc(inv_ps, 1)
            for _ in range(WARM):
                pe.matmul(bank[5][:, :], identb[:, :], mask[:, :], start=True, stop=True)
            pe.wait_ge(rvs_ok, 3)
            for n in range(NT):
                t = pe.matmul(bank[3][:, 0:3 * NT], ohoff[:, n, :], rvs[:, n, :, :].rearrange("p c k -> p (c k)"),
                              start=(n == 0), stop=(n == NT - 1))
            t.then_inc(scg_ps, 1)

            def rows(g):
                pe.wait_ge(xg_in[g], 16)
                if g >= 2:
                    pe.wait_ge(xs_ok, g - 1)
                pe.transpose(bank[6 + g % 2][:, 0:P], xg[:, g, D:2 * D], identf[:, :]).then_inc(xs_ps, 1)

            def up(q, at):
                pe.wait_ge(xs_ok, min(q, NT - 1) + 1)
                pe.wait_ge(w1_in[q % WBUF], 16 * (q // WBUF + 1))
                if q >= 3:
                    pe.wait_ge(hT_ok, FJ * (q - 2))
                for j in range(FJ):
                    t = pe.matmul(bank[q % 3][:, P * j:P * (j + 1)], w1c[:, q % WBUF, P * j:P * (j + 1)],
                                  xsT[:, bass.ds(at, P)], start=True, stop=True)
                t.then_inc(h_ps, 1)

            def down(q, ep_q):
                if q >= 2:
                    pe.wait_ge(yo_ok, q - 1)
                pe.matmul(bank[4 + q % 2][:, 0:D], sel[:, :, :].rearrange("p h s -> p (h s)")[:, bass.ds(ep_q, P)], b2p[:, :],
                          start=True, stop=False)
                for j in range(FJ):
                    pe.wait_ge(hT_ok, FJ * q + j + 1)
                    t = pe.matmul(bank[4 + q % 2][:, 0:D], hT[:, q % 2, j, :], w2_sb[:, bass.ds(ep_q * FJ + D * j, D)],
                                  start=False, stop=(j == FJ - 1))
                t.then_inc(y_ps, 1)

            pe.wait_ge(eq_ok, 2)
            pe.wait_ge(w2_in, 16)
            pe.wait_ge(b2c, 4)
            pe.wait_ge(sel_ok, 1)
            ep_q = before_q = at_q = 0
            rows(0)
            keep_warm(2, 5)
            for q in range(Q + 1):
                if q < Q:
                    up(q, at_q)
                if q + 1 < Q:
                    after_q = pe.value_load(ep[0:1, q + 1:q + 2], min_val=0, max_val=P * (E - 1))
                    at_q = nc.s_assert_within((q + 1) * P - after_q, 0, P * (NT - 1))
                if q + 1 < NT:
                    rows(q + 1)
                if q >= 1:
                    down(q - 1, before_q)
                before_q, ep_q = ep_q, after_q


_INS = ['x', 'ctx_1024', 'g_xattn', 'g_ffn', 'L0_xattn_igate_w', 'L0_xattn_igate_b', 'L0_xattn_fgate_w',
        'L0_xattn_fgate_b', 'L0_xattn_ln_scale', 'L0_ffn_switch_w', 'L0_ffn_switch_b', 'L0_ffn_w1', 'L0_ffn_b1',
        'L0_ffn_w2', 'L0_ffn_b2']
_OUTS = [((4, 256, 128), 'float32')]


def kernel(**inputs):
    import numpy as _np
    import concourse.bacc as _bacc
    from concourse import mybir as _mybir
    from concourse.bass_utils import run_bass_kernel_spmd as _run

    nc = _bacc.Bacc("TRN2", target_bir_lowering=False, num_devices=1)
    arrays, args = {}, []
    for name in _INS:
        a = _np.ascontiguousarray(inputs[name])
        arrays[f"in_{name}_dram"] = a
        args.append(nc.dram_tensor(f"in_{name}_dram", a.shape, _mybir.dt.from_np(a.dtype), kind="ExternalInput").ap())
    for i, (shape, dtype) in enumerate(_OUTS):
        dt = _mybir.dt.from_np(_np.dtype(dtype))
        args.append(nc.dram_tensor(f"out_{i}_dram", shape, dt, kind="ExternalOutput").ap())
    gated_block(nc, *args)
    r = _run(nc, [arrays], core_ids=[0])
    got = tuple(r.results[0][f"out_{i}_dram"] for i in range(len(_OUTS)))
    return got[0]
```
